# Optimizing a Trainium2 kernel written in Bass

```python
import numpy as np
import jax
import jax.numpy as jnp

def _softmax(x, axis=-1):
    return jax.nn.softmax(x, axis=axis)

def _gelu(x):
    return jax.nn.gelu(x, approximate=True)

def _silu(x):
    return jax.nn.silu(x)

def _sigmoid(x):
    return jax.nn.sigmoid(x)

def _layernorm(x, axis=-1, eps=1e-05):
    m = jnp.mean(x, axis=axis, keepdims=True)
    v = jnp.var(x, axis=axis, keepdims=True)
    return (x - m) / jnp.sqrt(v + eps)

def _scatter_add(tgt, idx, src, axis=0):
    return tgt.at[idx].add(src)

def _segment_sum(src, seg, n):
    return jax.ops.segment_sum(src, seg, n)
kernel_name = 'mk_cond_resid_d2_seqx_r8_5944b1'

def setup_inputs(seed: int=0):
    np.random.seed(seed)
    _w = jnp.asarray

    def _rec_inputs():
        import jax
        import jax.numpy as jnp
        _rk = jax.random.key(seed)
        x = -0.000125 + 0.9999 * jax.random.normal(jax.random.fold_in(_rk, 1), (64, 32, 512), jnp.float32)
        _lenS = 32 - jax.random.randint(jax.random.fold_in(_rk, 7), (64,), 0, max(1, 32 // 4) + 1, jnp.int32)
        _lenS2 = 32 - jax.random.randint(jax.random.fold_in(_rk, 8), (64,), 0, max(1, 32 // 4) + 1, jnp.int32)
        itok_B_6_15 = jax.random.randint(jax.random.fold_in(_rk, 11), (64,), 6, 16, jnp.int32)
        itok_B_2_6 = jax.random.randint(jax.random.fold_in(_rk, 12), (64,), 2, 7, jnp.int32)
        return (x, itok_B_6_15, itok_B_2_6)
    x, itok_B_6_15, itok_B_2_6 = _rec_inputs()

    def _L0_cond_setup():
        import jax, jax.numpy as jnp
        import numpy as np
        B, S, D_IN, D_OUT = (4, 256, 512, 512)
        RANK, MAX_LORAS = (16, 32)
        key = jax.random.key(seed)
        ks = jax.random.split(key, 6)
        x = jax.random.normal(ks[0], (B, S, D_IN), dtype=jnp.float32)
        adapter_ids = jax.random.randint(ks[1], (B,), 0, MAX_LORAS)
        base_weight = jax.random.normal(ks[2], (D_OUT, D_IN), dtype=jnp.float32) * D_IN ** (-0.5)
        base_bias = jax.random.normal(ks[3], (D_OUT,), dtype=jnp.float32) * 0.01
        lora_A_w = jax.random.normal(ks[4], (MAX_LORAS, RANK, D_IN), dtype=jnp.float32) * D_IN ** (-0.5)
        lora_B_w = jax.random.normal(ks[5], (MAX_LORAS, D_OUT, RANK), dtype=jnp.float32) * RANK ** (-0.5)
        return {'x': x, 'adapter_ids': adapter_ids, 'base_weight': base_weight, 'base_bias': base_bias, 'lora_A_w': lora_A_w, 'lora_B_w': lora_B_w}
    _L0_cond_all = _L0_cond_setup()
    _L0_cond_in = {k: v for k, v in _L0_cond_all.items() if k in ('base_weight', 'base_bias', 'lora_A_w', 'lora_B_w')}
    del _L0_cond_all

    def _L1_cond_setup():
        import jax, jax.numpy as jnp
        import numpy as np
        B, N, H, F = (4, 64, 512, 1376)
        L, R, RANK = (1, 16, 16)
        SCALE = 0.5
        key = jax.random.key(seed)
        ks = jax.random.split(key, 12)
        nrm = lambda k, shape, fan: jax.random.normal(k, shape, jnp.float32) * fan ** (-0.5)
        inp = {'x': jax.random.normal(ks[0], (B, N, H), jnp.float32), 'W_gate': nrm(ks[1], (F, H), H), 'W_up': nrm(ks[2], (F, H), H), 'W_down': nrm(ks[3], (H, F), F), 'A_gate': nrm(ks[4], (L, R, RANK, H), H), 'B_gate': nrm(ks[5], (L, R, F, RANK), RANK), 'A_up': nrm(ks[6], (L, R, RANK, H), H), 'B_up': nrm(ks[7], (L, R, F, RANK), RANK), 'A_down': nrm(ks[8], (L, R, RANK, F), F), 'B_down': nrm(ks[9], (L, R, H, RANK), RANK), 'lora_indices': jax.random.randint(ks[10], (B,), 0, R), 'layer_idx': 0}
        return inp
    _L1_cond_all = _L1_cond_setup()
    _L1_cond_in = {k: v for k, v in _L1_cond_all.items() if k in ('W_gate', 'W_up', 'W_down', 'A_gate', 'B_gate', 'A_up', 'B_up', 'A_down', 'B_down')}
    del _L1_cond_all
    return {'x': x, 'itok_B_6_15': itok_B_6_15, 'itok_B_2_6': itok_B_2_6, 'L0_cond_base_weight': _L0_cond_in['base_weight'], 'L0_cond_base_bias': _L0_cond_in['base_bias'], 'L0_cond_lora_A_w': _L0_cond_in['lora_A_w'], 'L0_cond_lora_B_w': _L0_cond_in['lora_B_w'], 'L1_cond_W_gate': _L1_cond_in['W_gate'], 'L1_cond_W_up': _L1_cond_in['W_up'], 'L1_cond_W_down': _L1_cond_in['W_down'], 'L1_cond_A_gate': _L1_cond_in['A_gate'], 'L1_cond_B_gate': _L1_cond_in['B_gate'], 'L1_cond_A_up': _L1_cond_in['A_up'], 'L1_cond_B_up': _L1_cond_in['B_up'], 'L1_cond_A_down': _L1_cond_in['A_down'], 'L1_cond_B_down': _L1_cond_in['B_down']}

def reference(x, itok_B_6_15, itok_B_2_6, L0_cond_base_weight, L0_cond_base_bias, L0_cond_lora_A_w, L0_cond_lora_B_w, L1_cond_W_gate, L1_cond_W_up, L1_cond_W_down, L1_cond_A_gate, L1_cond_B_gate, L1_cond_A_up, L1_cond_B_up, L1_cond_A_down, L1_cond_B_down):
    import jax
    import jax.numpy as jnp

    def _L0_cond_ref(x, adapter_ids, base_weight, base_bias, lora_A_w, lora_B_w):
        import jax, jax.numpy as jnp
        import numpy as np
        B, S, D_IN, D_OUT = (4, 256, 512, 512)
        RANK, MAX_LORAS = (16, 32)
        result = jnp.einsum('bsd,od->bso', x, base_weight) + base_bias
        A = lora_A_w[adapter_ids]
        Bw = lora_B_w[adapter_ids]
        h = jnp.einsum('bsd,brd->bsr', x, A)
        lora_out = jnp.einsum('bsr,bor->bso', h, Bw)
        result = result + lora_out
        return result.astype(x.dtype)

    def _L1_cond_ref(x, W_gate, W_up, W_down, A_gate, B_gate, A_up, B_up, A_down, B_down, lora_indices, layer_idx):
        import jax, jax.numpy as jnp
        import numpy as np
        B, N, H, F = (4, 64, 512, 1376)
        L, R, RANK = (1, 16, 16)
        SCALE = 0.5

        def lora_add(base, inp, A, B):
            Ab = A[layer_idx][lora_indices]
            Bb = B[layer_idx][lora_indices]
            t = jnp.einsum('bri,bni->bnr', Ab, inp)
            return base + jnp.einsum('bor,bnr->bno', Bb, t) * SCALE
        gate = lora_add(jnp.einsum('bnh,fh->bnf', x, W_gate), x, A_gate, B_gate)
        up = lora_add(jnp.einsum('bnh,fh->bnf', x, W_up), x, A_up, B_up)
        act = jax.nn.silu(gate) * up
        down = lora_add(jnp.einsum('bnf,hf->bnh', act, W_down), act, A_down, B_down)
        return down
    x = x + _L0_cond_ref(x, itok_B_6_15, L0_cond_base_weight, L0_cond_base_bias, L0_cond_lora_A_w, L0_cond_lora_B_w)
    x = x + _L1_cond_ref(x, L1_cond_W_gate, L1_cond_W_up, L1_cond_W_down, L1_cond_A_gate, L1_cond_B_gate, L1_cond_A_up, L1_cond_B_up, L1_cond_A_down, L1_cond_B_down, itok_B_2_6, 0)
    return x

_drawn_inputs = setup_inputs


def setup_inputs(seed=0):
    import zlib

    import numpy as np

    out = dict(_drawn_inputs(seed))
    spreads = {}
    factors = {'L0_cond_base_bias': 8.0}
    for name, (base, spread) in spreads.items():
        noise = np.random.default_rng([zlib.crc32(name.encode()), seed]).standard_normal(out[name].shape)
        drawn = base * np.exp(spread * noise) if base else spread * noise
        out[name] = jnp.asarray(drawn.astype(out[name].dtype))
    for name, factor in factors.items():
        out[name] = (out[name] * factor).astype(out[name].dtype)
    return out
```

```python
from contextlib import ExitStack

import concourse.bass as bass
from concourse import mybir

F32 = mybir.dt.float32
F32R = mybir.dt.float32r
I32 = mybir.dt.int32
U32 = mybir.dt.uint32
ALU = mybir.AluOpType
ACT = mybir.ActivationFunctionType
ds = bass.ds

P = 128
SEQ = 32
H = 512
KT = H // P
TOK = 512
NB = 4
SPB = TOK // SEQ
R = 16
GT = P // R * SEQ
NG = TOK // GT
F = 1376
J = -(-F // P)
SCALE = 0.5

NP = NQ = 4 + J + 1
NB_ = 1 + J + 1
ND = 1 + (J - 1) + 1
NA = KT + (J - 1)
UP_ = 4 + J
UQ_ = 3 + J
UA_ = KT + (J - 1)


def lora_ffn_program(nc, xT, w0, bias, a0, b0, wgu, wd, agu, bgu, ad, bd, ids, ids_rep, rank, mask, outT):
    ctx = ExitStack()
    with ctx:
        def sb(name, shape, dt=F32):
            return ctx.enter_context(nc.sbuf_tensor(name, shape, dt))

        def bank(name):
            return ctx.enter_context(nc.psum_tensor(name, [P, TOK], F32))

        def sem(name):
            return ctx.enter_context(nc.semaphore(name))

        def f32(t):
            return t.bitcast(F32)

        w0_raw = sb("w0_raw", [P, KT, H])
        wgu_raw = sb("wgu_raw", [P, J * 2, KT * P])
        wd_raw = sb("wd_raw", [P, J, H])
        bias_sb = sb("bias_sb", [P, KT])
        mask_sb = sb("mask_sb", [P, TOK])
        a0_raw = sb("a0_raw", [P, SPB, KT, R])
        agu_raw = sb("agu_raw", [P, SPB, 2, KT, R])
        ad_raw = sb("ad_raw", [P, SPB, J, R])
        bwide_raw = sb("bwide_raw", [P, NG, H])
        bgu_raw = sb("bgu_raw", [P, NG * 2 * P])
        tile_hi = {n: sb(f"{n}_hi", [P, 256 if n == "a" else 512], F32R) for n in "pqbda"}
        tile_lo = {n: sb(f"{n}_lo", [P, 256 if n == "a" else 512], F32R) for n in "pqbda"}
        x_raw = sb("x_raw", [P, KT, TOK])
        x_hi = sb("x_hi", [P, KT, TOK], F32R)
        x_lo = sb("x_lo", [P, KT, TOK], F32R)
        x1_raw = sb("x1_raw", [P, KT, TOK])
        x1_hi = sb("x1_hi", [P, KT, TOK], F32R)
        x1_lo = sb("x1_lo", [P, KT, TOK], F32R)
        silu_sb = sb("silu_sb", [P, TOK])
        h_raw = sb("h_raw", [P, TOK])
        h_hi = [sb(f"h_hi{i}", [P, TOK], F32R) for i in range(2)]
        h_lo = [sb(f"h_lo{i}", [P, TOK], F32R) for i in range(2)]
        t_raw = sb("t_raw", [P, TOK])
        t_hi = sb("t_hi", [P, TOK], F32R)
        t_lo = sb("t_lo", [P, TOK], F32R)
        tgu_raw = [sb(f"tgu_raw{s}", [P, TOK]) for s in range(2)]
        tgu_hi = [sb(f"tgu_hi{s}", [P, TOK], F32R) for s in range(2)]
        tgu_lo = [sb(f"tgu_lo{s}", [P, TOK], F32R) for s in range(2)]
        ids_sb = sb("ids_sb", [1, 2 * NB * SPB], I32)
        idrep_sb = sb("idrep_sb", [P, 2 * NB * NG], I32)
        rank_sb = sb("rank_sb", [P, 2 * NB * NG], I32)
        row_all = sb("row_all", [P, 2 * NB * NG], I32)
        row_b0 = sb("row_b0", [P, NG], I32)
        row_bd = sb("row_bd", [P, NG], I32)
        row_bgu = sb("row_bgu", [P, NG], I32)

        out_bank = [bank(f"out_bank{m}") for m in range(KT)]
        gate_bank = bank("gate_bank")
        up_bank = bank("up_bank")
        rank_bank = bank("rank_bank")
        rankgu_bank = bank("rankgu_bank")

        ids_in = sem("ids_in")
        rows_in = sem("rows_in")
        const_in = sem("const_in")
        x_in = sem("x_in")
        w0_in = sem("w0_in")
        wgu_in = sem("wgu_in")
        wd_in = sem("wd_in")
        a0_in = sem("a0_in")
        agu_in = sem("agu_in")
        ad_in = sem("ad_in")
        bwide_in = sem("bwide_in")
        bgu_in = sem("bgu_in")
        out_done = sem("out_done")
        hi_ready = {n: sem(f"{n}_hi_ready") for n in "pqbda"}
        lo_ready = {n: sem(f"{n}_lo_ready") for n in "pqbda"}
        tile_used = {n: sem(f"{n}_used") for n in "pqa"}
        x_hi_ready = sem("x_hi_ready")
        x_lo_ready = sem("x_lo_ready")
        l0_done = sem("l0_done")
        x1_raw_ready = sem("x1_raw_ready")
        x1_hi_ready = sem("x1_hi_ready")
        x1_lo_ready = sem("x1_lo_ready")
        rankgu_done = sem("rankgu_done")
        tgu_raw_ready = sem("tgu_raw_ready")
        tgu_hi_ready = sem("tgu_hi_ready")
        tgu_lo_ready = sem("tgu_lo_ready")
        rankd_done = sem("rankd_done")
        t_raw_ready = sem("t_raw_ready")
        t_hi_ready = sem("t_hi_ready")
        t_lo_ready = sem("t_lo_ready")
        gate_done = sem("gate_done")
        up_done = sem("up_done")
        silu_ready = sem("silu_ready")
        h_raw_ready = sem("h_raw_ready")
        h_hi_ready = sem("h_hi_ready")
        h_lo_ready = sem("h_lo_ready")
        down_done = sem("down_done")
        fin_done = sem("fin_done")
        bank_free = sem("bank_free")
        row_ready = sem("row_ready")
        zeroed = sem("zeroed")
        sp_passed = sem("sp_passed")
        pool_passed = sem("pool_passed")

        block = ctx.enter_context(nc.Block())

        @block.sync
        def _(sp):
            def gather(table, dst, arrived, first_id, adapters):
                width = table.shape[2]
                sp.wait_ge(ids_in, 16)
                sp.sem_inc(sp_passed)
                with sp.Fori(0, SPB) as s:
                    a = sp.value_load(ids_sb[0:1, ds(first_id + s, 1)], min_val=0, max_val=adapters - 1)
                    sp.dma_start(dst[:, ds(s * width, width)],
                                 table[ds(a, 1)].rearrange("a p c -> p (a c)")).then_inc(arrived, 16)

            a0_flat = a0_raw[:].rearrange("p s k r -> p (s k r)")
            agu_flat = agu_raw[:].rearrange("p s g k r -> p (s g k r)")
            ad_flat = ad_raw[:].rearrange("p s j r -> p (s j r)")
            first_l1 = NB * SPB

            sp.dma_start(ids_sb[:], ids).then_inc(ids_in, 16)
            sp.dma_start(x_raw[:], xT[0]).then_inc(x_in, 16)
            sp.dma_start(w0_raw[:], w0).then_inc(w0_in, 16)
            sp.dma_start(idrep_sb[:], ids_rep).then_inc(rows_in, 16)
            sp.dma_start(rank_sb[:], rank).then_inc(rows_in, 16)
            gather(a0, a0_flat, a0_in, 0, a0.shape[0])
            sp.dma_start(bias_sb[:], bias).then_inc(const_in, 16)
            sp.dma_start(mask_sb[:], mask).then_inc(const_in, 16)
            gather(agu, agu_flat, agu_in, first_l1, agu.shape[0])
            for j in range(J):
                if j:
                    sp.wait_ge(wgu_in, 16 * j)
                sp.dma_start(wgu_raw[:, 2 * j:2 * j + 2, :], wgu[:, 2 * j:2 * j + 2, :]).then_inc(wgu_in, 16)
                if j:
                    sp.wait_ge(wd_in, 16 * j)
                sp.dma_start(wd_raw[:, j, :], wd[:, j, :]).then_inc(wd_in, 16)
                if j == 0:
                    gather(ad, ad_flat, ad_in, first_l1, ad.shape[0])

            def store(b, m):
                sp.wait_ge(bank_free, KT + KT * b + m + 1)
                sp.dma_start(outT[ds(b, 1), :, m].rearrange("b p t -> p (b t)"), x1_raw[:, m, :]).then_inc(out_done, 16)

            with sp.Fori(0, NB - 1) as b:
                sp.wait_ge(x1_raw_ready, KT * (b + 1))
                sp.dma_start(x_raw[:], xT[ds(b + 1, 1)].rearrange("b p k t -> p (b k) t")).then_inc(x_in, 16)
                sp.wait_ge(lo_ready["a"], NA * b + KT)
                gather(a0, a0_flat, a0_in, (b + 1) * SPB, a0.shape[0])
                sp.wait_ge(lo_ready["p"], NP * b + 4)
                sp.wait_ge(lo_ready["q"], NQ * b + 4)
                gather(agu, agu_flat, agu_in, (b + 1) * SPB + first_l1, agu.shape[0])
                sp.wait_ge(lo_ready["q"], NQ * (b + 1))
                gather(ad, ad_flat, ad_in, (b + 1) * SPB + first_l1, ad.shape[0])
                for m in range(KT):
                    store(b, m)
            for m in range(KT):
                store(NB - 1, m)
            sp.wait_ge(out_done, 16 * NB * KT)

        @block.gpsimd
        def _(pool):
            def gather(dst, arrived, table, rows):
                nc.gpsimd.indirect_dma_start(dst, None, table, bass.IndirectOffsetOnAxis(rows.bitcast(U32), 0)
                                             ).then_inc(arrived, 16)

            pool.wait_ge(row_ready, 1)
            steps = 3 + (J - 1)
            with pool.Fori(0, NB) as b:
                if True:
                    pool.wait_ge(bgu_in, 16 * NG * J * b)
                    pool.wait_ge(bwide_in, 32 * NG * b)
                    nc.gpsimd.tensor_copy(row_b0[:], row_all[:, ds(NG * b, NG)]).then_inc(row_ready, 1)
                    nc.gpsimd.tensor_copy(row_bd[:], row_all[:, ds(NG * b + NB * NG, NG)]).then_inc(row_ready, 1)
                    nc.gpsimd.tensor_copy(row_bgu[:], row_all[:, ds(NG * b + NB * NG, NG)]).then_inc(row_ready, 1)
                pool.wait_ge(row_ready, 1 + steps * b + 3)
                pool.wait_ge(lo_ready["b"], NB_ * b)
                pool.wait_ge(lo_ready["d"], ND * b)
                pool.sem_inc(pool_passed)
                for g in range(NG):
                    gather(bwide_raw[:, g, :], bwide_in, b0, row_b0[:, g:g + 1])
                for g in range(NG):
                    gather(bgu_raw[:, g * 2 * P:(g + 1) * 2 * P], bgu_in, bgu, row_bgu[:, g:g + 1])
                pool.wait_ge(lo_ready["b"], NB_ * b + 1)
                pool.wait_ge(lo_ready["d"], ND * b + 1)
                pool.sem_inc(pool_passed)
                for g in range(NG):
                    gather(bwide_raw[:, g, :], bwide_in, bd, row_bd[:, g:g + 1])
                with pool.Fori(1, J) as j:
                    pool.wait_ge(bgu_in, 16 * NG * J * b + 16 * NG * j)
                    pool.sem_inc(pool_passed)
                    nc.gpsimd.tensor_scalar(row_bgu[:], row_bgu[:], float(bd.shape[0]), None, ALU.add).then_inc(row_ready, 1)
                    pool.wait_ge(row_ready, 1 + steps * b + 3 + j)
                    pool.wait_ge(lo_ready["b"], NB_ * b + 1 + j)
                    pool.sem_inc(pool_passed)
                    for g in range(NG):
                        gather(bgu_raw[:, g * 2 * P:(g + 1) * 2 * P], bgu_in, bgu, row_bgu[:, g:g + 1])

        def a0_cols(k):
            return a0_raw[:, :, k, :]

        def agu_cols(k, s):
            return agu_raw[:, :, s, k, :].rearrange("p (q c) r -> p q c r", c=4)

        def agu_place(t, s):
            return t[:].rearrange("p (q g c r) -> p q g c r", q=4, g=2, r=R)[:, :, s]

        def small_place(t):
            return t[:, 0:SPB * R].rearrange("p (s r) -> p s r", r=R)

        def ad_cols(j):
            if isinstance(j, int):
                return ad_raw[:, :, j, :]
            return ad_raw[:, :, ds(j, 1), :].rearrange("p s j r -> p s (j r)")

        def wd_cols(j):
            return wd_raw[:, j, :] if isinstance(j, int) else wd_raw[:, ds(j, 1), :].rearrange("p j n -> p (j n)")

        def wgu_cols(j, s):
            if isinstance(j, int):
                return wgu_raw[:, 2 * j + s, :]
            return wgu_raw[:, ds(j * 2 + s, 1), :].rearrange("p j n -> p (j n)")

        @block.scalar
        def _(act):
            def split(n, src, place=None):
                dst = tile_hi[n][:] if place is None else place(tile_hi[n])
                return nc.scalar.copy(dst, src)

            def x_block(b):
                act.wait_ge(x_in, 16 * (b + 1))
                act.wait_ge(tile_used["q"], UQ_ * b)
                for k in range(KT):
                    nc.scalar.copy(x_hi[:, k, :], x_raw[:, k, :]).then_inc(x_hi_ready, 1)

            def head(b):
                act.wait_ge(w0_in, 16)
                act.wait_ge(fin_done, KT * b)
                split("p", w0_raw[:, 0, :]).then_inc(hi_ready["p"], 1)
                split("q", w0_raw[:, 1, :]).then_inc(hi_ready["q"], 1)

            def head_a(b):
                act.wait_ge(a0_in, 16 * SPB * (b + 1))
                act.wait_ge(tile_used["a"], UA_ * b)
                split("a", a0_cols(0), small_place).then_inc(hi_ready["a"], 1)

            def fill_j(b, j):
                act.wait_ge(wgu_in, 16 * (j + 1))
                act.wait_ge(tile_used["p"], UP_ * b + 4 + j)
                split("p", wgu_cols(j, 0)).then_inc(hi_ready["p"], 1)
                return

            def fill_j2(b, j):
                act.wait_ge(bgu_in, 16 * NG * J * b + 16 * NG * (j + 1))
                split("b", bgu_raw[:]).then_inc(hi_ready["b"], 1)

            def silu(b, j):
                n = J * b + j
                act.wait_ge(gate_done, n + 1)
                act.wait_ge(h_raw_ready, n)
                nc.scalar.activation(silu_sb[:], gate_bank[:], ACT.Silu).then_inc(silu_ready, 1)

            def h_split(b, j, last):
                n = J * b + j
                act.wait_ge(h_raw_ready, n + 1)
                if not last:
                    act.wait_ge(down_done, n)
                nc.scalar.copy(h_hi[last][:], h_raw[:]).then_inc(h_hi_ready, 1)

            def body(b, last):
                act.wait_ge(tile_used["a"], UA_ * b + 1)
                split("a", a0_cols(1), small_place).then_inc(hi_ready["a"], 1)
                act.wait_ge(bwide_in, 32 * NG * b + 16 * NG)
                split("b", bwide_raw[:, 0, :]).then_inc(hi_ready["b"], 1)
                split("d", bwide_raw[:, 1, :]).then_inc(hi_ready["d"], 1)
                act.wait_ge(tile_used["p"], UP_ * b + 1)
                split("p", w0_raw[:, 2, :]).then_inc(hi_ready["p"], 1)
                act.wait_ge(tile_used["a"], UA_ * b + 2)
                split("a", a0_cols(2), small_place).then_inc(hi_ready["a"], 1)
                act.wait_ge(tile_used["q"], UQ_ * b + 1)
                split("q", w0_raw[:, 3, :]).then_inc(hi_ready["q"], 1)
                act.wait_ge(tile_used["a"], UA_ * b + 3)
                split("a", a0_cols(3), small_place).then_inc(hi_ready["a"], 1)

                act.wait_ge(agu_in, 16 * SPB * (b + 1))

                def gu_rows(n, k):
                    for s in range(2):
                        last_one = nc.scalar.copy(agu_place(tile_hi[n], s), agu_cols(k, s))
                    last_one.then_inc(hi_ready[n], 1)

                act.wait_ge(tile_used["p"], UP_ * b + 2)
                gu_rows("p", 0)
                act.wait_ge(t_raw_ready, 2 * b + 1)
                nc.scalar.copy(t_hi[:], t_raw[:]).then_inc(t_hi_ready, 1)
                act.wait_ge(tile_used["q"], UQ_ * b + 2)
                gu_rows("q", 1)
                for m in range(KT):
                    act.wait_ge(x1_raw_ready, KT * b + m + 1)
                    nc.scalar.copy(x1_hi[:, m, :], x1_raw[:, m, :]).then_inc(x1_hi_ready, 1)
                    if m == 1:
                        act.wait_ge(tile_used["p"], UP_ * b + 3)
                        gu_rows("p", 2)
                    if m == 2:
                        act.wait_ge(tile_used["q"], UQ_ * b + 3)
                        gu_rows("q", 3)
                fill_j(b, 0)
                for s in range(2):
                    act.wait_ge(tgu_raw_ready, 2 * b + s + 1)
                    nc.scalar.copy(tgu_hi[s][:], tgu_raw[s][:]).then_inc(tgu_hi_ready, 1)
                act.wait_ge(rankgu_done, b + 1)
                split("q", wgu_cols(0, 1)).then_inc(hi_ready["q"], 1)
                act.wait_ge(l0_done, KT * (b + 1))
                fill_j2(b, 0)

                with act.Fori(0, J - 1) as j:
                    silu(b, j)
                    fill_j(b, j + 1)
                    act.wait_ge(tile_used["q"], UQ_ * b + 3 + j + 1)
                    split("q", wgu_cols(j + 1, 1)).then_inc(hi_ready["q"], 1)
                    act.wait_ge(up_done, J * b + j + 1)
                    fill_j2(b, j + 1)
                    h_split(b, j, 0)
                    act.wait_ge(wd_in, 16 * (j + 1))
                    act.wait_ge(l0_done, KT * (b + 1))
                    act.wait_ge(down_done, J * b + j)
                    split("d", wd_cols(j)).then_inc(hi_ready["d"], 1)
                    act.wait_ge(ad_in, 16 * SPB * (b + 1))
                    act.wait_ge(tile_used["a"], UA_ * b + KT + j)
                    split("a", ad_cols(j), small_place).then_inc(hi_ready["a"], 1)

                silu(b, J - 1)
                act.wait_ge(wd_in, 16 * J)
                act.wait_ge(tile_used["p"], UP_ * b + 4 + J)
                split("p", wd_cols(J - 1)).then_inc(hi_ready["p"], 1)
                if not last:
                    x_block(b + 1)
                act.wait_ge(tile_used["q"], UQ_ * b + 3 + J)
                split("q", ad_cols(J - 1), small_place).then_inc(hi_ready["q"], 1)
                act.wait_ge(bwide_in, 32 * NG * (b + 1))
                act.wait_ge(up_done, J * (b + 1))
                split("b", bwide_raw[:, 0, :]).then_inc(hi_ready["b"], 1)
                h_split(b, J - 1, 1)
                if not last:
                    head_a(b + 1)
                act.wait_ge(down_done, J * b + J - 1)
                split("d", bwide_raw[:, 1, :]).then_inc(hi_ready["d"], 1)
                act.wait_ge(t_raw_ready, 2 * b + 2)
                act.wait_ge(l0_done, KT * (b + 1))
                nc.scalar.copy(t_hi[:], t_raw[:]).then_inc(t_hi_ready, 1)
                if not last:
                    act.wait_ge(down_done, J * (b + 1))
                    split("p", w0_raw[:, 0, :]).then_inc(hi_ready["p"], 1)
                    split("q", w0_raw[:, 1, :]).then_inc(hi_ready["q"], 1)

            x_block(0)
            act.wait_ge(w0_in, 16)
            split("p", w0_raw[:, 0, :]).then_inc(hi_ready["p"], 1)
            split("q", w0_raw[:, 1, :]).then_inc(hi_ready["q"], 1)
            head_a(0)
            with act.Fori(0, NB - 1) as b:
                body(b, False)
            body(NB - 1, True)

        @block.vector
        def _(dve):
            def rest(n, src, place=None, count=None):
                dst, hi = (tile_lo[n][:], f32(tile_hi[n][:])) if place is None else \
                    (place(tile_lo[n]), f32(place(tile_hi[n])))
                dve.wait_ge(hi_ready[n], count)
                return nc.vector.tensor_tensor(dst, src, hi, ALU.subtract)

            def x_block(b):
                for k in range(KT):
                    dve.wait_ge(x_hi_ready, KT * b + k + 1)
                    nc.vector.tensor_tensor(x_lo[:, k, :], x_raw[:, k, :], f32(x_hi[:, k, :]),
                                            ALU.subtract).then_inc(x_lo_ready, 1)

            def head(b):
                rest("p", w0_raw[:, 0, :], count=NP * b + 1).then_inc(lo_ready["p"], 1)
                rest("q", w0_raw[:, 1, :], count=NQ * b + 1).then_inc(lo_ready["q"], 1)

            def head_a(b):
                rest("a", a0_cols(0), small_place, NA * b + 1).then_inc(lo_ready["a"], 1)

            def t_ranks(n):
                dve.wait_ge(t_lo_ready, n)
                nc.vector.tensor_tensor(t_raw[:], rank_bank[:], mask_sb[:], ALU.mult).then_inc(t_raw_ready, 1)

            def h_product(b, j):
                n = J * b + j
                dve.wait_ge(silu_ready, n + 1)
                dve.wait_ge(up_done, n + 1)
                dve.wait_ge(h_lo_ready, n)
                nc.vector.tensor_tensor(h_raw[:], up_bank[:], silu_sb[:], ALU.mult).then_inc(h_raw_ready, 1)

            def h_rest(b, j, last):
                dve.wait_ge(h_hi_ready, J * b + j + 1)
                nc.vector.tensor_tensor(h_lo[last][:], h_raw[:], f32(h_hi[last][:]),
                                        ALU.subtract).then_inc(h_lo_ready, 1)

            def body(b, last):
                rest("a", a0_cols(1), small_place, NA * b + 2).then_inc(lo_ready["a"], 1)
                rest("b", bwide_raw[:, 0, :], count=NB_ * b + 1).then_inc(lo_ready["b"], 1)
                rest("d", bwide_raw[:, 1, :], count=ND * b + 1).then_inc(lo_ready["d"], 1)
                rest("p", w0_raw[:, 2, :], count=NP * b + 2).then_inc(lo_ready["p"], 1)
                rest("a", a0_cols(2), small_place, NA * b + 3).then_inc(lo_ready["a"], 1)
                rest("q", w0_raw[:, 3, :], count=NQ * b + 2).then_inc(lo_ready["q"], 1)
                rest("a", a0_cols(3), small_place, NA * b + 4).then_inc(lo_ready["a"], 1)

                def gu_rows(n, k, count):
                    dve.wait_ge(hi_ready[n], count)
                    for s in range(2):
                        last_one = nc.vector.tensor_tensor(agu_place(tile_lo[n], s), agu_cols(k, s),
                                                           f32(agu_place(tile_hi[n], s)), ALU.subtract)
                    last_one.then_inc(lo_ready[n], 1)

                gu_rows("p", 0, NP * b + 3)
                dve.wait_ge(tile_used["a"], UA_ * b + KT)
                t_ranks(2 * b)
                dve.wait_ge(t_hi_ready, 2 * b + 1)
                nc.vector.tensor_tensor(t_lo[:], t_raw[:], f32(t_hi[:]), ALU.subtract).then_inc(t_lo_ready, 1)
                gu_rows("q", 1, NQ * b + 3)
                for m in range(KT):
                    dve.wait_ge(l0_done, KT * b + m + 1)
                    dve.wait_ge(out_done, 16 * KT * b)
                    nc.vector.scalar_tensor_tensor(x1_raw[:, m, :], out_bank[m][:], bias_sb[:, m:m + 1],
                                                   x_raw[:, m, :], ALU.add, ALU.add).then_inc(x1_raw_ready, 1)
                    dve.wait_ge(x1_hi_ready, KT * b + m + 1)
                    nc.vector.tensor_tensor(x1_lo[:, m, :], x1_raw[:, m, :], f32(x1_hi[:, m, :]),
                                            ALU.subtract).then_inc(x1_lo_ready, 1)
                    if m == 1:
                        gu_rows("p", 2, NP * b + 4)
                    if m == 2:
                        gu_rows("q", 3, NQ * b + 4)
                rest("p", wgu_cols(0, 0), count=NP * b + 5).then_inc(lo_ready["p"], 1)
                dve.wait_ge(rankgu_done, b + 1)
                dve.wait_ge(tgu_lo_ready, 2 * b)
                for s in range(2):
                    for odd in range(2):
                        rows, own = slice(64 * s, 64 * s + 64), slice(64 * odd, 64 * odd + 64)
                        cols = lambda t, h: t.rearrange("p (g h t) -> p g h t", h=2, t=P)[:, :, h, :]
                        last_one = nc.vector.scalar_tensor_tensor(
                            cols(tgu_raw[s][own, :], odd), cols(rankgu_bank[rows, :], odd), SCALE,
                            cols(mask_sb[rows, :], s), ALU.mult, ALU.mult)
                    last_one.then_inc(tgu_raw_ready, 1)
                for s in range(2):
                    dve.wait_ge(tgu_hi_ready, 2 * b + s + 1)
                    nc.vector.tensor_tensor(tgu_lo[s][:], tgu_raw[s][:], f32(tgu_hi[s][:]),
                                            ALU.subtract).then_inc(tgu_lo_ready, 1)
                rest("q", wgu_cols(0, 1), count=NQ * b + 5).then_inc(lo_ready["q"], 1)
                rest("b", bgu_raw[:], count=NB_ * b + 2).then_inc(lo_ready["b"], 1)

                with dve.Fori(0, J - 1) as j:
                    rest("p", wgu_cols(j + 1, 0), count=NP * b + 6 + j).then_inc(lo_ready["p"], 1)
                    h_product(b, j)
                    rest("q", wgu_cols(j + 1, 1), count=NQ * b + 6 + j).then_inc(lo_ready["q"], 1)
                    rest("b", bgu_raw[:], count=NB_ * b + 3 + j).then_inc(lo_ready["b"], 1)
                    h_rest(b, j, 0)
                    rest("d", wd_cols(j), count=ND * b + 2 + j).then_inc(lo_ready["d"], 1)
                    rest("a", ad_cols(j), small_place, NA * b + KT + 1 + j).then_inc(lo_ready["a"], 1)

                rest("p", wd_cols(J - 1), count=NP * (b + 1)).then_inc(lo_ready["p"], 1)
                if not last:
                    x_block(b + 1)
                h_product(b, J - 1)
                rest("q", ad_cols(J - 1), small_place, NQ * (b + 1)).then_inc(lo_ready["q"], 1)
                rest("b", bwide_raw[:, 0, :], count=NB_ * (b + 1)).then_inc(lo_ready["b"], 1)
                h_rest(b, J - 1, 1)
                if not last:
                    head_a(b + 1)
                rest("d", bwide_raw[:, 1, :], count=ND * (b + 1)).then_inc(lo_ready["d"], 1)
                dve.wait_ge(rankd_done, b + 1)
                dve.wait_ge(t_lo_ready, 2 * b + 1)
                nc.vector.scalar_tensor_tensor(t_raw[:], rank_bank[:], SCALE, mask_sb[:],
                                               ALU.mult, ALU.mult).then_inc(t_raw_ready, 1)
                dve.wait_ge(t_hi_ready, 2 * b + 2)
                nc.vector.tensor_tensor(t_lo[:], t_raw[:], f32(t_hi[:]), ALU.subtract).then_inc(t_lo_ready, 1)
                if not last:
                    head(b + 1)
                for m in range(KT):
                    dve.wait_ge(fin_done, KT * b + m + 1)
                    nc.vector.tensor_tensor(x1_raw[:, m, :], out_bank[m][:], x1_raw[:, m, :],
                                            ALU.add).then_inc(bank_free, 1)

            dve.wait_ge(rows_in, 32)
            nc.vector.tensor_scalar(row_all[:], idrep_sb[:], float(R), None, ALU.mult).then_inc(zeroed, 1)
            dve.wait_ge(zeroed, 1)
            nc.vector.tensor_tensor(row_all[:], row_all[:], rank_sb[:], ALU.add).then_inc(row_ready, 1)
            for s in range(2):
                nc.vector.memset(tgu_raw[s][:], 0.0).then_inc(zeroed, 1)
            dve.wait_ge(zeroed, 3)
            x_block(0)
            head(0)
            head_a(0)
            dve.wait_ge(const_in, 32)
            nc.vector.memset(t_raw[:, 0:1], 0.0).then_inc(bank_free, KT)
            with dve.Fori(0, NB - 1) as b:
                body(b, False)
            body(NB - 1, True)

        @block.tensor
        def _(pe):
            def mm3(out, w_hi, w_lo, v_hi, v_lo, start=False, stop=False):
                nc.tensor.matmul(out, w_lo, v_hi, start=start, stop=False, skip_group_check=True)
                nc.tensor.matmul(out, w_hi, v_lo, start=False, stop=False, skip_group_check=True)
                return nc.tensor.matmul(out, w_hi, v_hi, start=False, stop=stop, skip_group_check=True)

            def group(g):
                return slice(g * GT, (g + 1) * GT)

            def col(n, c, w=P):
                return tile_hi[n][:, c:c + w], tile_lo[n][:, c:c + w]

            def gate_up(b, j):
                pe.wait_ge(lo_ready["p"], NP * b + 5 + j)
                pe.wait_ge(silu_ready, J * b + j)
                for k in range(KT):
                    last_one = mm3(gate_bank[:], *col("p", k * P), x1_hi[:, k, :], x1_lo[:, k, :], start=(k == 0))
                last_one.then_inc(tile_used["p"], 1)
                pe.wait_ge(lo_ready["b"], NB_ * b + 2 + j)
                for s, out_ in enumerate((gate_bank, up_bank)):
                    if s == 1:
                        pe.wait_ge(lo_ready["q"], NQ * b + 5 + j)
                        pe.wait_ge(h_raw_ready, J * b + j)
                        for k in range(KT):
                            last_one = mm3(up_bank[:], *col("q", k * P), x1_hi[:, k, :], x1_lo[:, k, :], start=(k == 0))
                        last_one.then_inc(tile_used["q"], 1)
                    pe.wait_ge(tgu_lo_ready, 2 * b + s + 1)
                    for g in range(NG):
                        last_one = mm3(out_[:, group(g)], *col("b", (2 * g + s) * P),
                                       tgu_hi[s][:, group(g)], tgu_lo[s][:, group(g)], stop=(g == NG - 1))
                    last_one.then_inc((gate_done, up_done)[s], 1)

            def down(b, j, first, last):
                a, w = ("q", "p") if last else ("a", "d")
                pe.wait_ge(h_lo_ready, J * b + j + 1)
                if last:
                    pe.wait_ge(lo_ready["q"], NQ * (b + 1))
                else:
                    pe.wait_ge(lo_ready["a"], NA * b + KT + 1 + j)
                for g in range(NG):
                    last_one = mm3(rank_bank[:, group(g)], *col(a, g * P), h_hi[last][:, group(g)],
                                   h_lo[last][:, group(g)], start=(first and g == 0), stop=bool(last and g == NG - 1))
                last_one.then_inc(rankd_done if last else tile_used["a"], 1)
                if last:
                    pe.wait_ge(lo_ready["p"], NP * (b + 1))
                else:
                    pe.wait_ge(lo_ready["d"], ND * b + 2 + j)
                for m in range(KT):
                    last_one = mm3(out_bank[m][:], *col(w, m * P), h_hi[last][:], h_lo[last][:], start=first)
                last_one.then_inc(down_done, 1)

            def b_rows(done):
                for m in range(KT):
                    for g, n in enumerate("bd"):
                        last_one = mm3(out_bank[m][:, group(g)], *col(n, m * P), t_hi[:, group(g)],
                                       t_lo[:, group(g)], stop=(g == NG - 1))
                    last_one.then_inc(done, 1)

            def body(b):
                for k in range(KT):
                    n = "pq"[k % 2]
                    pe.wait_ge(x_lo_ready, KT * b + k + 1)
                    pe.wait_ge(lo_ready["a"], NA * b + k + 1)
                    for g in range(NG):
                        last_one = mm3(rank_bank[:, group(g)], *col("a", g * P), x_hi[:, k, group(g)],
                                       x_lo[:, k, group(g)], start=(k == 0 and g == 0),
                                       stop=(k == KT - 1 and g == NG - 1))
                    last_one.then_inc(tile_used["a"], 1)
                    pe.wait_ge(lo_ready[n], (NP if n == "p" else NQ) * b + k // 2 + 1)
                    for m in range(KT):
                        if k == 0:
                            pe.wait_ge(bank_free, KT * b + m + 1)
                        last_one = mm3(out_bank[m][:], *col(n, m * P), x_hi[:, k, :], x_lo[:, k, :], start=(k == 0))
                    last_one.then_inc(tile_used[n], 1)
                pe.wait_ge(lo_ready["b"], NB_ * b + 1)
                pe.wait_ge(lo_ready["d"], ND * b + 1)
                pe.wait_ge(t_lo_ready, 2 * b + 1)
                b_rows(l0_done)
                for k in range(KT):
                    n = "pq"[k % 2]
                    pe.wait_ge(x1_lo_ready, KT * b + k + 1)
                    pe.wait_ge(lo_ready[n], (NP if n == "p" else NQ) * b + 3 + k // 2)
                    for q in range(TOK // P):
                        cols = slice(q * P, (q + 1) * P)
                        last_one = mm3(rankgu_bank[:, cols], *col(n, q * P), x1_hi[:, k, cols], x1_lo[:, k, cols],
                                       start=(k == 0 and q == 0), stop=(k == KT - 1 and q == TOK // P - 1))
                    last_one.then_inc(rankgu_done if k == KT - 1 else tile_used[n], 1)
                gate_up(b, 0)
                gate_up(b, 1)
                down(b, 0, True, 0)
                with pe.Fori(2, J) as j:
                    gate_up(b, j)
                    down(b, j - 1, False, 0)
                down(b, J - 1, False, 1)
                pe.wait_ge(lo_ready["b"], NB_ * (b + 1))
                pe.wait_ge(lo_ready["d"], ND * (b + 1))
                pe.wait_ge(t_lo_ready, 2 * b + 2)
                b_rows(fin_done)

            with pe.Fori(0, NB) as b:
                body(b)


def kernel(**inputs):
    import numpy as np
    import concourse.bacc as bacc
    from concourse.bass_utils import run_bass_kernel_spmd

    def tiles(w):
        return w.reshape(w.shape[0], -1, P).transpose(2, 1, 0)

    def pad(w, axis):
        widths = [(0, 0)] * w.ndim
        widths[axis] = (0, J * P - w.shape[axis])
        return np.pad(w, widths)

    v = {k: np.asarray(a) for k, a in inputs.items()}
    x = v["x"]
    nseq = x.shape[0]
    c = {n[len("L1_cond_"):]: a for n, a in v.items() if n.startswith("L1_cond_")}
    gate, up = (pad(c[n], 0).reshape(J, P, KT, P) for n in ("W_gate", "W_up"))
    a_gate, a_up = (c[n][0].reshape(-1, R, KT, P) for n in ("A_gate", "A_up"))
    b_gate, b_up = (pad(c[n][0], 1).reshape(-1, J, P, R) for n in ("B_gate", "B_up"))
    ids = np.concatenate([v["itok_B_6_15"], v["itok_B_2_6"]])
    per_group = P // R
    own = np.arange(P)[:, None] // R == (np.arange(TOK)[None, :] // SEQ) % per_group
    arrays = {
        "xT": x.reshape(NB, TOK, KT, P).transpose(0, 3, 2, 1),
        "w0": tiles(v["L0_cond_base_weight"]),
        "bias": v["L0_cond_base_bias"].reshape(KT, P).T,
        "a0": v["L0_cond_lora_A_w"].reshape(-1, R, KT, P).transpose(0, 3, 2, 1).reshape(-1, P, KT * R),
        "b0": v["L0_cond_lora_B_w"].transpose(0, 2, 1).reshape(-1, H),
        "wgu": np.stack([gate, up]).transpose(4, 1, 0, 3, 2).reshape(P, J * 2, KT * P),
        "wd": tiles(pad(c["W_down"], 1)),
        "agu": np.stack([a_gate, a_up]).transpose(1, 4, 0, 3, 2).reshape(-1, P, 2 * KT * R),
        "bgu": np.stack([b_gate, b_up]).transpose(2, 1, 4, 0, 3).reshape(-1, 2 * P),
        "ad": pad(c["A_down"][0], 2).reshape(-1, R, J, P).transpose(0, 3, 2, 1).reshape(-1, P, J * R),
        "bd": c["B_down"][0].transpose(0, 2, 1).reshape(-1, H),
        "ids": ids.reshape(1, -1),
        "ids_rep": np.repeat(ids.reshape(-1, per_group), R, axis=1).T,
        "rank": np.tile((np.arange(P, dtype=np.int32) % R)[:, None], (1, 2 * nseq // per_group)),
        "mask": own.astype(np.float32),
    }
    nc = bacc.Bacc("TRN2", target_bir_lowering=False, num_devices=1)
    arrays = {f"{n}_dram": np.ascontiguousarray(a) for n, a in arrays.items()}
    aps = [nc.dram_tensor(n, a.shape, mybir.dt.from_np(a.dtype), kind="ExternalInput").ap() for n, a in arrays.items()]
    out = nc.dram_tensor("out_dram", (NB, P, KT, TOK), F32, kind="ExternalOutput").ap()
    lora_ffn_program(nc, *aps, out)
    r = run_bass_kernel_spmd(nc, [arrays], core_ids=[0])
    got = r.results[0]["out_dram"]
    return got.transpose(0, 3, 2, 1).reshape(x.shape)
```

```python
from contextlib import ExitStack

import concourse.bass as bass
from concourse import mybir

F32 = mybir.dt.float32
F32R = mybir.dt.float32r
I32 = mybir.dt.int32
U32 = mybir.dt.uint32
ALU = mybir.AluOpType
ACT = mybir.ActivationFunctionType
ds = bass.ds

P = 128
SEQ = 32
H = 512
KT = H // P
TOK = 512
NB = 4
SPB = TOK // SEQ
R = 16
GT = P // R * SEQ
NG = TOK // GT
F = 1376
J = -(-F // P)
SCALE = 0.5

NP = NQ = 3 + J + 1
NB_ = 1 + J + 1
ND = 1 + (J - 1) + 1
NA = KT + (J - 1)
UP_ = UQ_ = 3 + J
UA_ = KT + (J - 1)


def wait_after(engine, semaphore, count):
    if not (isinstance(count, int) and count == 0):
        engine.wait_ge(semaphore, count)


def lora_ffn_program(nc, xT, w0, bias, a0, b0, wgu, wd, agu, bgu, ad, bd, ids, seq_rows, group_rows, mask, outT):
    ctx = ExitStack()
    with ctx:
        def sb(name, shape, dt=F32):
            return ctx.enter_context(nc.sbuf_tensor(name, shape, dt))

        def bank(name):
            return ctx.enter_context(nc.psum_tensor(name, [P, TOK], F32))

        def sem(name):
            return ctx.enter_context(nc.semaphore(name))

        def f32(t):
            return t.bitcast(F32)

        w0_raw = sb("w0_raw", [P, KT, H])
        wgu_raw = sb("wgu_raw", [P, J * 2, KT * P])
        wd_raw = sb("wd_raw", [P, J, H])
        bias_sb = sb("bias_sb", [P, KT])
        mask_sb = sb("mask_sb", [P, TOK])
        a0_raw = sb("a0_raw", [P, SPB, KT, R])
        agu_raw = sb("agu_raw", [P, SPB, 2, KT, R])
        ad_raw = sb("ad_raw", [P, SPB, J, R])
        bwide_raw = sb("bwide_raw", [P, NG, H])
        bgu_raw = sb("bgu_raw", [P, NG * 2 * P])
        tile_hi = {n: sb(f"{n}_hi", [P, 256 if n == "a" else 512], F32R) for n in "pqbda"}
        tile_lo = {n: sb(f"{n}_lo", [P, 256 if n == "a" else 512], F32R) for n in "pqbda"}
        x_raw = sb("x_raw", [P, KT, TOK])
        x_hi = sb("x_hi", [P, KT, TOK], F32R)
        x_lo = sb("x_lo", [P, KT, TOK], F32R)
        x1_raw = sb("x1_raw", [P, KT, TOK])
        x1_hi = sb("x1_hi", [P, KT, TOK], F32R)
        x1_lo = sb("x1_lo", [P, KT, TOK], F32R)
        silu_sb = sb("silu_sb", [P, TOK])
        h_raw = sb("h_raw", [P, TOK])
        h_hi = [sb(f"h_hi{i}", [P, TOK], F32R) for i in range(2)]
        h_lo = [sb(f"h_lo{i}", [P, TOK], F32R) for i in range(2)]
        t_raw = sb("t_raw", [P, TOK])
        t_hi = sb("t_hi", [P, TOK], F32R)
        t_lo = sb("t_lo", [P, TOK], F32R)
        tgu_raw = [sb(f"tgu_raw{s}", [P, TOK]) for s in range(2)]
        tgu_hi = [sb(f"tgu_hi{s}", [P, TOK], F32R) for s in range(2)]
        tgu_lo = [sb(f"tgu_lo{s}", [P, TOK], F32R) for s in range(2)]
        ids_sb = sb("ids_sb", [1, 2 * NB * SPB], I32)
        group_sb = sb("group_sb", [P, 2, 2 * NB * NG], I32)
        seq_sb = sb("seq_sb", [P, 2, SPB], I32)
        row_b0 = sb("row_b0", [P, NG], I32)
        row_bd = sb("row_bd", [P, NG], I32)
        row_bgu = sb("row_bgu", [P, NG], I32)

        out_bank = [bank(f"out_bank{m}") for m in range(KT)]
        gate_bank = bank("gate_bank")
        up_bank = bank("up_bank")
        rank_bank = bank("rank_bank")
        rankgu_bank = bank("rankgu_bank")

        ids_in = sem("ids_in")
        rows_in = sem("rows_in")
        const_in = sem("const_in")
        x_in = sem("x_in")
        w0_in = sem("w0_in")
        wgu_in = sem("wgu_in")
        wd_in = sem("wd_in")
        a0_first_in = sem("a0_first_in")
        a0_in = sem("a0_in")
        agu_in = sem("agu_in")
        ad_in = sem("ad_in")
        bwide_in = sem("bwide_in")
        bgu_in = sem("bgu_in")
        out_done = sem("out_done")
        hi_ready = {n: sem(f"{n}_hi_ready") for n in "pqbda"}
        lo_ready = {n: sem(f"{n}_lo_ready") for n in "pqbda"}
        tile_used = {n: sem(f"{n}_used") for n in "pqa"}
        x_hi_ready = sem("x_hi_ready")
        x_lo_ready = sem("x_lo_ready")
        l0_done = sem("l0_done")
        x1_raw_ready = sem("x1_raw_ready")
        x1_hi_ready = sem("x1_hi_ready")
        x1_lo_ready = sem("x1_lo_ready")
        rankgu_done = sem("rankgu_done")
        tgu_raw_ready = sem("tgu_raw_ready")
        tgu_hi_ready = sem("tgu_hi_ready")
        tgu_lo_ready = sem("tgu_lo_ready")
        rankd_done = sem("rankd_done")
        t_raw_ready = sem("t_raw_ready")
        t_hi_ready = sem("t_hi_ready")
        t_lo_ready = sem("t_lo_ready")
        gate_done = sem("gate_done")
        up_done = sem("up_done")
        silu_ready = sem("silu_ready")
        h_raw_ready = sem("h_raw_ready")
        h_hi_ready = sem("h_hi_ready")
        h_lo_ready = sem("h_lo_ready")
        hrow_hi_ready = sem("hrow_hi_ready")
        hrow_lo_ready = sem("hrow_lo_ready")
        down_done = sem("down_done")
        fin_done = sem("fin_done")
        bank_free = sem("bank_free")
        row_ready = sem("row_ready")
        zeroed = sem("zeroed")
        sp_passed = sem("sp_passed")
        pool_passed = sem("pool_passed")

        block = ctx.enter_context(nc.Block())

        @block.sync
        def _(sp):
            def gather(table, dst, arrived, first):
                width = table.shape[2]
                sp.sem_inc(sp_passed)
                with sp.Fori(0, SPB) as s:
                    a = sp.value_load(ids_sb[0:1, ds(first + s, 1)], min_val=0, max_val=table.shape[0] - 1)
                    sp.dma_start(dst[:, ds(s * width, width)],
                                 table[ds(a, 1)].rearrange("a p c -> p (a c)")).then_inc(arrived, 16)

            l1 = NB * SPB
            a0_tab = a0.rearrange("(a p) c -> a p c", p=P)
            a0_flat = a0_raw[:].rearrange("p s k r -> p (s k r)")
            agu_flat = agu_raw[:].rearrange("p s g k r -> p (s g k r)")
            ad_flat = ad_raw[:].rearrange("p s j r -> p (s j r)")

            sp.dma_start(ids_sb[:], ids).then_inc(ids_in, 16)
            sp.dma_start(group_sb[:], group_rows).then_inc(rows_in, 16)
            sp.dma_start(seq_sb[:], seq_rows).then_inc(rows_in, 16)
            sp.dma_start(x_raw[:], xT[0]).then_inc(x_in, 16)
            sp.dma_start(w0_raw[:], w0).then_inc(w0_in, 16)
            sp.dma_start(mask_sb[:], mask).then_inc(const_in, 16)
            sp.dma_start(bias_sb[:], bias).then_inc(const_in, 16)
            sp.dma_start(wgu_raw[:, 0:2, :], wgu[:, 0:2, :]).then_inc(wgu_in, 16)
            sp.dma_start(wd_raw[:, 0, :], wd[:, 0, :]).then_inc(wd_in, 16)
            sp.wait_ge(ids_in, 16)
            gather(agu, agu_flat, agu_in, l1)
            gather(ad, ad_flat, ad_in, l1)
            for j in range(1, J):
                sp.wait_ge(wgu_in, 16 * j)
                sp.dma_start(wgu_raw[:, 2 * j:2 * j + 2, :], wgu[:, 2 * j:2 * j + 2, :]).then_inc(wgu_in, 16)
                sp.wait_ge(wd_in, 16 * j)
                sp.dma_start(wd_raw[:, j, :], wd[:, j, :]).then_inc(wd_in, 16)

            def store(b, m):
                sp.wait_ge(bank_free, KT + KT * b + m + 1)
                sp.sem_inc(sp_passed)
                sp.dma_start(outT[ds(b, 1), :, m].rearrange("b p t -> p (b t)"), x1_raw[:, m, :]).then_inc(out_done, 16)

            def load_next(b):
                sp.wait_ge(x1_raw_ready, KT * (b + 1))
                sp.sem_inc(sp_passed)
                sp.dma_start(x_raw[:], xT[ds(b + 1, 1)].rearrange("b p k t -> p (b k) t")).then_inc(x_in, 16)
                sp.wait_ge(lo_ready["a"], NA * b + KT)
                gather(a0_tab, a0_flat, a0_in, (b + 1) * SPB)
                sp.wait_ge(hrow_lo_ready, 2 * (b + 1))
                sp.sem_inc(sp_passed)
                sp.wait_ge(lo_ready["p"], NP * b + 3)
                sp.wait_ge(lo_ready["q"], NQ * b + 3)
                gather(agu, agu_flat, agu_in, (b + 1) * SPB + l1)
                for m in range(KT):
                    store(b, m)
                sp.wait_ge(lo_ready["q"], NQ * (b + 1))
                gather(ad, ad_flat, ad_in, (b + 1) * SPB + l1)

            load_next(0)
            with sp.Fori(1, NB - 1) as b:
                load_next(b)
            for m in range(KT):
                store(NB - 1, m)
            sp.wait_ge(out_done, 16 * NB * KT)

        @block.gpsimd
        def _(pool):
            def gather(dst, arrived, table, rows):
                nc.gpsimd.indirect_dma_start(dst, None, table, bass.IndirectOffsetOnAxis(rows.bitcast(U32), 0)
                                             ).then_inc(arrived, 16)

            def gather_a0():
                for i in range(SPB):
                    gather(a0_raw[:, i].rearrange("p k r -> p (k r)"), a0_first_in, a0, seq_sb[:, 0, i:i + 1])

            def gather_wide(table, rows):
                for g in range(NG):
                    gather(bwide_raw[:, g, :], bwide_in, table, rows[:, g:g + 1])

            def gather_gu():
                for g in range(NG):
                    gather(bgu_raw[:, g * 2 * P:(g + 1) * 2 * P], bgu_in, bgu, row_bgu[:, g:g + 1])

            steps = 3 + (J - 1)

            def body(b):
                wait_after(pool, bgu_in, 16 * NG * J * b)
                wait_after(pool, bwide_in, 32 * NG * b)
                pool.sem_inc(pool_passed)
                for rows, src, first, n in ((row_b0, group_sb[:, 0], 0, NG),
                                            (row_bgu, group_sb[:, 0], NB * NG, NG), (row_bd, group_sb[:, 0], NB * NG, NG)):
                    nc.gpsimd.tensor_copy(rows[:], src[:, ds(b * n + first, n)]).then_inc(row_ready, 1)
                pool.wait_ge(row_ready, 2 + steps * b + 3)
                wait_after(pool, lo_ready["b"], NB_ * b)
                wait_after(pool, lo_ready["d"], ND * b)
                pool.sem_inc(pool_passed)
                gather_wide(b0, row_b0)
                gather_gu()
                pool.wait_ge(lo_ready["b"], NB_ * b + 1)
                pool.wait_ge(lo_ready["d"], ND * b + 1)
                pool.sem_inc(pool_passed)
                gather_wide(bd, row_bd)
                with pool.Fori(1, J) as j:
                    pool.wait_ge(bgu_in, 16 * NG * J * b + 16 * NG * j)
                    pool.sem_inc(pool_passed)
                    nc.gpsimd.tensor_scalar(row_bgu[:], row_bgu[:], float(bd.shape[0]), None, ALU.add).then_inc(row_ready, 1)
                    pool.wait_ge(row_ready, 2 + steps * b + 3 + j)
                    pool.wait_ge(lo_ready["b"], NB_ * b + 1 + j)
                    pool.sem_inc(pool_passed)
                    gather_gu()

            pool.wait_ge(row_ready, 2)
            gather_a0()
            body(0)
            with pool.Fori(1, NB) as b:
                body(b)

        def a0_cols(k):
            return a0_raw[:, :, k, :]

        def agu_cols(k, s):
            return agu_raw[:, :, s, k, :].rearrange("p (q c) r -> p q c r", c=4)

        def agu_place(t, s):
            return t[:].rearrange("p (q g c r) -> p q g c r", q=4, g=2, r=R)[:, :, s]

        def small_place(t):
            return t[:, 0:SPB * R].rearrange("p (s r) -> p s r", r=R)

        def ad_cols(j):
            if isinstance(j, int):
                return ad_raw[:, :, j, :]
            return ad_raw[:, :, ds(j, 1), :].rearrange("p s j r -> p s (j r)")

        def wd_cols(j):
            return wd_raw[:, j, :] if isinstance(j, int) else wd_raw[:, ds(j, 1), :].rearrange("p j n -> p (j n)")

        def wgu_cols(j, s):
            if isinstance(j, int):
                return wgu_raw[:, 2 * j + s, :]
            return wgu_raw[:, ds(j * 2 + s, 1), :].rearrange("p j n -> p (j n)")

        @block.scalar
        def _(act):
            def split(n, src, place=None):
                dst = tile_hi[n][:] if place is None else place(tile_hi[n])
                return nc.scalar.copy(dst, src)

            def x_split(b, k):
                nc.scalar.copy(x_hi[:, k, :], x_raw[:, k, :]).then_inc(x_hi_ready, 1)

            def gu_rows(dst, k, ready):
                for s in range(2):
                    last_one = nc.scalar.copy(agu_place(dst, s), agu_cols(k, s))
                last_one.then_inc(ready, 1)

            def silu(b, j):
                n = J * b + j
                act.wait_ge(gate_done, n + 1)
                wait_after(act, h_raw_ready, n)
                nc.scalar.activation(silu_sb[:], gate_bank[:], ACT.Silu).then_inc(silu_ready, 1)

            def next_gate(b, j):
                act.wait_ge(wgu_in, 16 * (j + 1))
                act.wait_ge(tile_used["p"], UP_ * b + 3 + j)
                split("p", wgu_cols(j, 0)).then_inc(hi_ready["p"], 1)

            def next_up(b, j):
                act.wait_ge(tile_used["q"], UQ_ * b + 3 + j)
                split("q", wgu_cols(j, 1)).then_inc(hi_ready["q"], 1)

            def next_b_rows(b, j):
                act.wait_ge(bgu_in, 16 * NG * J * b + 16 * NG * (j + 1))
                split("b", bgu_raw[:]).then_inc(hi_ready["b"], 1)

            def h_split(b, j, last):
                act.wait_ge(h_raw_ready, J * b + j + 1)
                nc.scalar.copy(h_hi[last][:], h_raw[:]).then_inc(h_hi_ready, 1)

            def tile_step(b, j):
                silu(b, j)
                next_gate(b, j + 1)
                next_up(b, j + 1)
                act.wait_ge(up_done, J * b + j + 1)
                next_b_rows(b, j + 1)
                wait_after(act, down_done, J * b + j)
                act.wait_ge(l0_done, KT * (b + 1))
                act.wait_ge(rankgu_done, b + 1)
                h_split(b, j, 0)
                act.wait_ge(wd_in, 16 * (j + 1))
                split("d", wd_cols(j)).then_inc(hi_ready["d"], 1)
                act.wait_ge(ad_in, 16 * SPB * (b + 1))
                act.wait_ge(tile_used["a"], UA_ * b + KT + j)
                split("a", ad_cols(j), small_place).then_inc(hi_ready["a"], 1)

            def body(b, last):
                act.wait_ge(tile_used["p"], UP_ * b + 1)
                split("p", w0_raw[:, 2, :]).then_inc(hi_ready["p"], 1)
                if isinstance(b, int) and b == 0:
                    act.wait_ge(a0_first_in, 16 * SPB)
                    split("a", a0_cols(0), small_place).then_inc(hi_ready["a"], 1)
                act.wait_ge(bwide_in, 32 * NG * b + 16 * NG)
                split("b", bwide_raw[:, 0, :]).then_inc(hi_ready["b"], 1)
                split("d", bwide_raw[:, 1, :]).then_inc(hi_ready["d"], 1)
                act.wait_ge(tile_used["q"], UQ_ * b + 1)
                split("q", w0_raw[:, 3, :]).then_inc(hi_ready["q"], 1)
                for k in range(1, KT):
                    act.wait_ge(tile_used["a"], UA_ * b + k)
                    split("a", a0_cols(k), small_place).then_inc(hi_ready["a"], 1)
                act.wait_ge(agu_in, 16 * SPB * (b + 1))
                wait_after(act, down_done, J * b)
                gu_rows(h_hi[0], 2, hrow_hi_ready)
                gu_rows(h_hi[1], 3, hrow_hi_ready)
                act.wait_ge(tile_used["p"], UP_ * b + 2)
                gu_rows(tile_hi["p"], 0, hi_ready["p"])
                act.wait_ge(t_raw_ready, 2 * b + 1)
                nc.scalar.copy(t_hi[:], t_raw[:]).then_inc(t_hi_ready, 1)
                act.wait_ge(tile_used["q"], UQ_ * b + 2)
                gu_rows(tile_hi["q"], 1, hi_ready["q"])
                for m in range(KT):
                    act.wait_ge(x1_raw_ready, KT * b + m + 1)
                    nc.scalar.copy(x1_hi[:, m, :], x1_raw[:, m, :]).then_inc(x1_hi_ready, 1)
                next_gate(b, 0)
                act.wait_ge(l0_done, KT * (b + 1))
                next_b_rows(b, 0)
                next_up(b, 0)
                for s in range(2):
                    act.wait_ge(tgu_raw_ready, 2 * b + s + 1)
                    nc.scalar.copy(tgu_hi[s][:], tgu_raw[s][:]).then_inc(tgu_hi_ready, 1)
                tile_step(b, 0)
                with act.Fori(1, J - 1) as j:
                    tile_step(b, j)
                silu(b, J - 1)
                act.wait_ge(wd_in, 16 * J)
                act.wait_ge(tile_used["p"], UP_ * (b + 1))
                split("p", wd_cols(J - 1)).then_inc(hi_ready["p"], 1)
                if not last:
                    act.wait_ge(x_in, 16 * (b + 2))
                    act.wait_ge(l0_done, KT * (b + 1))
                    x_split(b + 1, 0)
                act.wait_ge(tile_used["q"], UQ_ * (b + 1))
                split("q", ad_cols(J - 1), small_place).then_inc(hi_ready["q"], 1)
                h_split(b, J - 1, 1)
                act.wait_ge(bwide_in, 32 * NG * (b + 1))
                act.wait_ge(up_done, J * (b + 1))
                split("b", bwide_raw[:, 0, :]).then_inc(hi_ready["b"], 1)
                act.wait_ge(down_done, J * b + J - 1)
                split("d", bwide_raw[:, 1, :]).then_inc(hi_ready["d"], 1)
                act.wait_ge(t_raw_ready, 2 * b + 2)
                act.wait_ge(l0_done, KT * (b + 1))
                nc.scalar.copy(t_hi[:], t_raw[:]).then_inc(t_hi_ready, 1)
                if not last:
                    x_split(b + 1, 1)
                    act.wait_ge(down_done, J * (b + 1))
                    split("p", w0_raw[:, 0, :]).then_inc(hi_ready["p"], 1)
                    split("q", w0_raw[:, 1, :]).then_inc(hi_ready["q"], 1)
                    act.wait_ge(a0_in, 16 * SPB * (b + 1))
                    act.wait_ge(tile_used["a"], UA_ * (b + 1))
                    split("a", a0_cols(0), small_place).then_inc(hi_ready["a"], 1)
                    x_split(b + 1, 2)
                    x_split(b + 1, 3)

            act.wait_ge(zeroed, 1)
            nc.scalar.activation(silu_sb[:, 0:1], tgu_raw[0][:, 0:1], ACT.Silu)
            act.wait_ge(x_in, 16)
            x_split(0, 0)
            x_split(0, 1)
            act.wait_ge(w0_in, 16)
            split("p", w0_raw[:, 0, :]).then_inc(hi_ready["p"], 1)
            split("q", w0_raw[:, 1, :]).then_inc(hi_ready["q"], 1)
            x_split(0, 2)
            x_split(0, 3)
            body(0, False)
            with act.Fori(1, NB - 1) as b:
                body(b, False)
            body(NB - 1, True)

        @block.vector
        def _(dve):
            def rest(n, src, place=None, count=None):
                dst, hi = (tile_lo[n][:], f32(tile_hi[n][:])) if place is None else \
                    (place(tile_lo[n]), f32(place(tile_hi[n])))
                dve.wait_ge(hi_ready[n], count)
                return nc.vector.tensor_tensor(dst, src, hi, ALU.subtract)

            def x_rest(b, k):
                dve.wait_ge(x_hi_ready, KT * b + k + 1)
                nc.vector.tensor_tensor(x_lo[:, k, :], x_raw[:, k, :], f32(x_hi[:, k, :]),
                                        ALU.subtract).then_inc(x_lo_ready, 1)

            def gu_rows(lo, hi, k, made, count, ready):
                dve.wait_ge(made, count)
                for s in range(2):
                    last_one = nc.vector.tensor_tensor(agu_place(lo, s), agu_cols(k, s), f32(agu_place(hi, s)),
                                                       ALU.subtract)
                last_one.then_inc(ready, 1)

            def h_product(b, j):
                n = J * b + j
                dve.wait_ge(silu_ready, n + 1)
                dve.wait_ge(up_done, n + 1)
                wait_after(dve, h_lo_ready, n)
                nc.vector.tensor_tensor(h_raw[:], up_bank[:], silu_sb[:], ALU.mult).then_inc(h_raw_ready, 1)

            def h_rest(b, j, last):
                dve.wait_ge(h_hi_ready, J * b + j + 1)
                nc.vector.tensor_tensor(h_lo[last][:], h_raw[:], f32(h_hi[last][:]),
                                        ALU.subtract).then_inc(h_lo_ready, 1)

            def t_rest(n):
                dve.wait_ge(t_hi_ready, n)
                nc.vector.tensor_tensor(t_lo[:], t_raw[:], f32(t_hi[:]), ALU.subtract).then_inc(t_lo_ready, 1)

            def x1_sum(b, m):
                dve.wait_ge(l0_done, KT * b + m + 1)
                nc.vector.scalar_tensor_tensor(x1_raw[:, m, :], out_bank[m][:], bias_sb[:, m:m + 1],
                                               x_raw[:, m, :], ALU.add, ALU.add).then_inc(x1_raw_ready, 1)

            def x1_rest(b, m):
                dve.wait_ge(x1_hi_ready, KT * b + m + 1)
                nc.vector.tensor_tensor(x1_lo[:, m, :], x1_raw[:, m, :], f32(x1_hi[:, m, :]),
                                        ALU.subtract).then_inc(x1_lo_ready, 1)

            def final_sum(b, m):
                dve.wait_ge(fin_done, KT * b + m + 1)
                nc.vector.tensor_tensor(x1_raw[:, m, :], out_bank[m][:], x1_raw[:, m, :],
                                        ALU.add).then_inc(bank_free, 1)

            def tile_step(b, j):
                rest("p", wgu_cols(j + 1, 0), count=NP * b + 5 + j).then_inc(lo_ready["p"], 1)
                h_product(b, j)
                rest("q", wgu_cols(j + 1, 1), count=NQ * b + 5 + j).then_inc(lo_ready["q"], 1)
                rest("b", bgu_raw[:], count=NB_ * b + 3 + j).then_inc(lo_ready["b"], 1)
                h_rest(b, j, 0)
                rest("d", wd_cols(j), count=ND * b + 2 + j).then_inc(lo_ready["d"], 1)
                rest("a", ad_cols(j), small_place, NA * b + KT + 1 + j).then_inc(lo_ready["a"], 1)

            def body(b, last):
                rest("p", w0_raw[:, 2, :], count=NP * b + 2).then_inc(lo_ready["p"], 1)
                if isinstance(b, int) and b == 0:
                    rest("a", a0_cols(0), small_place, 1).then_inc(lo_ready["a"], 1)
                rest("b", bwide_raw[:, 0, :], count=NB_ * b + 1).then_inc(lo_ready["b"], 1)
                rest("d", bwide_raw[:, 1, :], count=ND * b + 1).then_inc(lo_ready["d"], 1)
                rest("q", w0_raw[:, 3, :], count=NQ * b + 2).then_inc(lo_ready["q"], 1)
                for k in range(1, KT):
                    rest("a", a0_cols(k), small_place, NA * b + k + 1).then_inc(lo_ready["a"], 1)
                gu_rows(h_lo[0], h_hi[0], 2, hrow_hi_ready, 2 * b + 1, hrow_lo_ready)
                gu_rows(h_lo[1], h_hi[1], 3, hrow_hi_ready, 2 * b + 2, hrow_lo_ready)
                gu_rows(tile_lo["p"], tile_hi["p"], 0, hi_ready["p"], NP * b + 3, lo_ready["p"])
                dve.wait_ge(tile_used["a"], UA_ * b + KT)
                wait_after(dve, t_lo_ready, 2 * b)
                nc.vector.tensor_tensor(t_raw[:], rank_bank[:], mask_sb[:], ALU.mult).then_inc(t_raw_ready, 1)
                t_rest(2 * b + 1)
                gu_rows(tile_lo["q"], tile_hi["q"], 1, hi_ready["q"], NQ * b + 3, lo_ready["q"])
                wait_after(dve, out_done, 16 * KT * b)
                x1_sum(b, 0)
                for m in range(1, KT):
                    x1_sum(b, m)
                    x1_rest(b, m - 1)
                x1_rest(b, KT - 1)
                rest("p", wgu_cols(0, 0), count=NP * b + 4).then_inc(lo_ready["p"], 1)
                rest("b", bgu_raw[:], count=NB_ * b + 2).then_inc(lo_ready["b"], 1)
                rest("q", wgu_cols(0, 1), count=NQ * b + 4).then_inc(lo_ready["q"], 1)
                dve.wait_ge(rankgu_done, b + 1)
                wait_after(dve, tgu_lo_ready, 2 * b)
                for s in range(2):
                    for odd in range(2):
                        rows, own = slice(64 * s, 64 * s + 64), slice(64 * odd, 64 * odd + 64)
                        cols = lambda t, h: t.rearrange("p (g h t) -> p g h t", h=2, t=P)[:, :, h, :]
                        last_one = nc.vector.scalar_tensor_tensor(
                            cols(tgu_raw[s][own, :], odd), cols(rankgu_bank[rows, :], odd), SCALE,
                            cols(mask_sb[rows, :], s), ALU.mult, ALU.mult)
                    last_one.then_inc(tgu_raw_ready, 1)
                for s in range(2):
                    dve.wait_ge(tgu_hi_ready, 2 * b + s + 1)
                    nc.vector.tensor_tensor(tgu_lo[s][:], tgu_raw[s][:], f32(tgu_hi[s][:]),
                                            ALU.subtract).then_inc(tgu_lo_ready, 1)
                tile_step(b, 0)
                with dve.Fori(1, J - 1) as j:
                    tile_step(b, j)

                rest("p", wd_cols(J - 1), count=NP * (b + 1)).then_inc(lo_ready["p"], 1)
                if not last:
                    x_rest(b + 1, 0)
                h_product(b, J - 1)
                rest("q", ad_cols(J - 1), small_place, NQ * (b + 1)).then_inc(lo_ready["q"], 1)
                h_rest(b, J - 1, 1)
                rest("b", bwide_raw[:, 0, :], count=NB_ * (b + 1)).then_inc(lo_ready["b"], 1)
                dve.wait_ge(rankd_done, b + 1)
                dve.wait_ge(t_lo_ready, 2 * b + 1)
                nc.vector.scalar_tensor_tensor(t_raw[:], rank_bank[:], SCALE, mask_sb[:],
                                               ALU.mult, ALU.mult).then_inc(t_raw_ready, 1)
                rest("d", bwide_raw[:, 1, :], count=ND * (b + 1)).then_inc(lo_ready["d"], 1)
                t_rest(2 * b + 2)
                if not last:
                    x_rest(b + 1, 1)
                    rest("p", w0_raw[:, 0, :], count=NP * (b + 1) + 1).then_inc(lo_ready["p"], 1)
                final_sum(b, 0)
                if not last:
                    rest("q", w0_raw[:, 1, :], count=NQ * (b + 1) + 1).then_inc(lo_ready["q"], 1)
                final_sum(b, 1)
                if not last:
                    rest("a", a0_cols(0), small_place, NA * (b + 1) + 1).then_inc(lo_ready["a"], 1)
                    x_rest(b + 1, 2)
                final_sum(b, 2)
                if not last:
                    x_rest(b + 1, 3)
                final_sum(b, 3)

            for s in range(2):
                nc.vector.memset(tgu_raw[s][:], 0.0).then_inc(zeroed, 1)
            nc.vector.memset(t_raw[:, 0:1], 0.0).then_inc(bank_free, KT)
            dve.wait_ge(rows_in, 32)
            for t, rows in ((seq_sb, P), (group_sb, R)):
                nc.vector.scalar_tensor_tensor(t[:, 0], t[:, 0], float(rows), t[:, 1],
                                               ALU.mult, ALU.add).then_inc(row_ready, 1)
            dve.wait_ge(zeroed, 2)
            x_rest(0, 0)
            x_rest(0, 1)
            rest("p", w0_raw[:, 0, :], count=1).then_inc(lo_ready["p"], 1)
            rest("q", w0_raw[:, 1, :], count=1).then_inc(lo_ready["q"], 1)
            x_rest(0, 2)
            x_rest(0, 3)
            dve.wait_ge(const_in, 32)
            body(0, False)
            with dve.Fori(1, NB - 1) as b:
                body(b, False)
            body(NB - 1, True)

        @block.tensor
        def _(pe):
            def mm3(out, w_hi, w_lo, v_hi, v_lo, start=False, stop=False):
                nc.tensor.matmul(out, w_lo, v_hi, start=start, stop=False, skip_group_check=True)
                nc.tensor.matmul(out, w_hi, v_lo, start=False, stop=False, skip_group_check=True)
                return nc.tensor.matmul(out, w_hi, v_hi, start=False, stop=stop, skip_group_check=True)

            def group(g):
                return slice(g * GT, (g + 1) * GT)

            def col(n, c, w=P):
                return tile_hi[n][:, c:c + w], tile_lo[n][:, c:c + w]

            def gate_up(b, j):
                pe.wait_ge(lo_ready["p"], NP * b + 4 + j)
                wait_after(pe, silu_ready, J * b + j)
                for k in range(KT):
                    last_one = mm3(gate_bank[:], *col("p", k * P), x1_hi[:, k, :], x1_lo[:, k, :], start=(k == 0))
                last_one.then_inc(tile_used["p"], 1)
                pe.wait_ge(lo_ready["b"], NB_ * b + 2 + j)
                for s, out_ in enumerate((gate_bank, up_bank)):
                    if s == 1:
                        pe.wait_ge(lo_ready["q"], NQ * b + 4 + j)
                        wait_after(pe, h_raw_ready, J * b + j)
                        for k in range(KT):
                            last_one = mm3(up_bank[:], *col("q", k * P), x1_hi[:, k, :], x1_lo[:, k, :], start=(k == 0))
                        last_one.then_inc(tile_used["q"], 1)
                    pe.wait_ge(tgu_lo_ready, 2 * b + s + 1)
                    for g in range(NG):
                        last_one = mm3(out_[:, group(g)], *col("b", (2 * g + s) * P),
                                       tgu_hi[s][:, group(g)], tgu_lo[s][:, group(g)], stop=(g == NG - 1))
                    last_one.then_inc((gate_done, up_done)[s], 1)

            def down(b, j, first, last):
                a, w = ("q", "p") if last else ("a", "d")
                pe.wait_ge(h_lo_ready, J * b + j + 1)
                if last:
                    pe.wait_ge(lo_ready["q"], NQ * (b + 1))
                else:
                    pe.wait_ge(lo_ready["a"], NA * b + KT + 1 + j)
                for g in range(NG):
                    last_one = mm3(rank_bank[:, group(g)], *col(a, g * P), h_hi[last][:, group(g)],
                                   h_lo[last][:, group(g)], start=(first and g == 0), stop=bool(last and g == NG - 1))
                last_one.then_inc(rankd_done if last else tile_used["a"], 1)
                if last:
                    pe.wait_ge(lo_ready["p"], NP * (b + 1))
                else:
                    pe.wait_ge(lo_ready["d"], ND * b + 2 + j)
                for m in range(KT):
                    last_one = mm3(out_bank[m][:], *col(w, m * P), h_hi[last][:], h_lo[last][:], start=first)
                last_one.then_inc(down_done, 1)

            def b_rows(done):
                for m in range(KT):
                    for g, n in enumerate("bd"):
                        last_one = mm3(out_bank[m][:, group(g)], *col(n, m * P), t_hi[:, group(g)],
                                       t_lo[:, group(g)], stop=(g == NG - 1))
                    last_one.then_inc(done, 1)

            def w0_rows(b, k, tiles):
                n = "pq"[k % 2]
                pe.wait_ge(x_lo_ready, KT * b + k + 1)
                pe.wait_ge(lo_ready[n], (NP if n == "p" else NQ) * b + k // 2 + 1)
                for m in tiles:
                    if k == 0:
                        pe.wait_ge(bank_free, KT * b + m + 1)
                    last_one = mm3(out_bank[m][:], *col(n, m * P), x_hi[:, k, :], x_lo[:, k, :], start=(k == 0))
                if m == KT - 1:
                    last_one.then_inc(tile_used[n], 1)

            def ranks0(b, k):
                pe.wait_ge(lo_ready["a"], NA * b + k + 1)
                for g in range(NG):
                    last_one = mm3(rank_bank[:, group(g)], *col("a", g * P), x_hi[:, k, group(g)],
                                   x_lo[:, k, group(g)], start=(k == 0 and g == 0),
                                   stop=(k == KT - 1 and g == NG - 1))
                last_one.then_inc(tile_used["a"], 1)

            def body(b):
                w0_rows(b, 0, range(KT))
                w0_rows(b, 1, range(KT))
                ranks0(b, 0)
                w0_rows(b, 2, range(0, 2))
                ranks0(b, 1)
                w0_rows(b, 2, range(2, KT))
                ranks0(b, 2)
                w0_rows(b, 3, range(0, 2))
                ranks0(b, 3)
                w0_rows(b, 3, range(2, KT))
                pe.wait_ge(lo_ready["b"], NB_ * b + 1)
                pe.wait_ge(lo_ready["d"], ND * b + 1)
                pe.wait_ge(t_lo_ready, 2 * b + 1)
                b_rows(l0_done)
                rows = [(tile_hi["p"], tile_lo["p"], lo_ready["p"], NP * b + 3),
                        (tile_hi["q"], tile_lo["q"], lo_ready["q"], NQ * b + 3),
                        (h_hi[0], h_lo[0], hrow_lo_ready, 2 * b + 1),
                        (h_hi[1], h_lo[1], hrow_lo_ready, 2 * b + 2)]
                for k, (hi, lo, made, count) in enumerate(rows):
                    pe.wait_ge(x1_lo_ready, KT * b + k + 1)
                    pe.wait_ge(made, count)
                    for q in range(TOK // P):
                        cols = slice(q * P, (q + 1) * P)
                        last_one = mm3(rankgu_bank[:, cols], hi[:, cols], lo[:, cols], x1_hi[:, k, cols],
                                       x1_lo[:, k, cols], start=(k == 0 and q == 0),
                                       stop=(k == KT - 1 and q == TOK // P - 1))
                    if k < 2:
                        last_one.then_inc(tile_used["pq"[k]], 1)
                last_one.then_inc(rankgu_done, 1)
                gate_up(b, 0)
                gate_up(b, 1)
                down(b, 0, True, 0)
                with pe.Fori(2, J) as j:
                    gate_up(b, j)
                    down(b, j - 1, False, 0)
                down(b, J - 1, False, 1)
                pe.wait_ge(lo_ready["b"], NB_ * (b + 1))
                pe.wait_ge(lo_ready["d"], ND * (b + 1))
                pe.wait_ge(t_lo_ready, 2 * b + 2)
                b_rows(fin_done)

            body(0)
            with pe.Fori(1, NB) as b:
                body(b)


def kernel(**inputs):
    import numpy as np
    import concourse.bacc as bacc
    from concourse.bass_utils import run_bass_kernel_spmd

    def tiles(w):
        return w.reshape(w.shape[0], -1, P).transpose(2, 1, 0)

    def pad(w, axis):
        widths = [(0, 0)] * w.ndim
        widths[axis] = (0, J * P - w.shape[axis])
        return np.pad(w, widths)

    v = {k: np.asarray(a) for k, a in inputs.items()}
    x = v["x"]
    nseq = x.shape[0]
    c = {n[len("L1_cond_"):]: a for n, a in v.items() if n.startswith("L1_cond_")}
    gate, up = (pad(c[n], 0).reshape(J, P, KT, P) for n in ("W_gate", "W_up"))
    a_gate, a_up = (c[n][0].reshape(-1, R, KT, P) for n in ("A_gate", "A_up"))
    b_gate, b_up = (pad(c[n][0], 1).reshape(-1, J, P, R) for n in ("B_gate", "B_up"))
    ids0, ids1 = v["itok_B_6_15"], v["itok_B_2_6"]
    place = np.arange(P, dtype=np.int32)[:, None]
    per_group = P // R
    own = np.arange(P)[:, None] // R == (np.arange(TOK)[None, :] // SEQ) % per_group
    arrays = {
        "xT": x.reshape(NB, TOK, KT, P).transpose(0, 3, 2, 1),
        "w0": tiles(v["L0_cond_base_weight"]),
        "bias": v["L0_cond_base_bias"].reshape(KT, P).T,
        "a0": v["L0_cond_lora_A_w"].reshape(-1, R, KT, P).transpose(0, 3, 2, 1).reshape(-1, KT * R),
        "b0": v["L0_cond_lora_B_w"].transpose(0, 2, 1).reshape(-1, H),
        "wgu": np.stack([gate, up]).transpose(4, 1, 0, 3, 2).reshape(P, J * 2, KT * P),
        "wd": tiles(pad(c["W_down"], 1)),
        "agu": np.stack([a_gate, a_up]).transpose(1, 4, 0, 3, 2).reshape(-1, P, 2 * KT * R),
        "bgu": np.stack([b_gate, b_up]).transpose(2, 1, 4, 0, 3).reshape(-1, 2 * P),
        "ad": pad(c["A_down"][0], 2).reshape(-1, R, J, P).transpose(0, 3, 2, 1).reshape(-1, P, J * R),
        "bd": c["B_down"][0].transpose(0, 2, 1).reshape(-1, H),
        "ids": np.concatenate([ids0, ids1]).reshape(1, -1),
        "seq_rows": np.stack([np.tile(ids0[:SPB], (P, 1)), np.tile(place, (1, SPB))], axis=1),
        "group_rows": np.stack([np.repeat(np.concatenate([ids0, ids1]).reshape(-1, per_group), R, axis=1).T,
                                np.tile(place % R, (1, 2 * nseq // per_group))], axis=1),
        "mask": own.astype(np.float32),
    }
    nc = bacc.Bacc("TRN2", target_bir_lowering=False, num_devices=1)
    arrays = {f"{n}_dram": np.ascontiguousarray(a) for n, a in arrays.items()}
    aps = [nc.dram_tensor(n, a.shape, mybir.dt.from_np(a.dtype), kind="ExternalInput").ap() for n, a in arrays.items()]
    out = nc.dram_tensor("out_dram", (NB, P, KT, TOK), F32, kind="ExternalOutput").ap()
    lora_ffn_program(nc, *aps, out)
    r = run_bass_kernel_spmd(nc, [arrays], core_ids=[0])
    got = r.results[0]["out_dram"]
    return got.transpose(0, 3, 2, 1).reshape(x.shape)
```

```python
from contextlib import ExitStack

import concourse.bass as bass
from concourse import mybir

F32 = mybir.dt.float32
F32R = mybir.dt.float32r
I32 = mybir.dt.int32
U32 = mybir.dt.uint32
ALU = mybir.AluOpType
ACT = mybir.ActivationFunctionType
ds = bass.ds

P = 128
SEQ = 32
H = 512
KT = H // P
TOK = 512
NB = 4
SPB = TOK // SEQ
R = 16
GT = P // R * SEQ
NG = TOK // GT
F = 1376
J = -(-F // P)
SCALE = 0.5

NP = NQ = 3 + J + 1
NB_ = 1 + J + 1
ND = 1 + (J - 1) + 1
NA = KT + (J - 1)
UP_ = 3 + J
UQ_ = 2 + J
UA_ = NA
POOL_A0, POOL_AGU, ACT_AGU, POOL_AD = 8, 5, 5, 6


def wait_after(engine, semaphore, count):
    if not (isinstance(count, int) and count == 0):
        engine.wait_ge(semaphore, count)


def lora_ffn_program(nc, xT, w0, bias, a0, b0, wgu, wd, agu, bgu, ad, bd, ids, seq_rows, group_rows, mask, outT):
    ctx = ExitStack()
    with ctx:
        def sb(name, shape, dt=F32):
            return ctx.enter_context(nc.sbuf_tensor(name, shape, dt))

        def bank(name):
            return ctx.enter_context(nc.psum_tensor(name, [P, TOK], F32))

        def sem(name):
            return ctx.enter_context(nc.semaphore(name))

        def f32(t):
            return t.bitcast(F32)

        w0_raw = sb("w0_raw", [P, KT, H])
        wgu_raw = sb("wgu_raw", [P, J * 2, KT * P])
        wd_raw = sb("wd_raw", [P, J, H])
        bias_sb = sb("bias_sb", [P, KT])
        mask_sb = sb("mask_sb", [P, TOK])
        a0_raw = sb("a0_raw", [P, SPB, KT, R])
        agu_raw = sb("agu_raw", [P, SPB, 2, KT, R])
        ad_raw = sb("ad_raw", [P, SPB, J, R])
        bwide_raw = sb("bwide_raw", [P, NG, H])
        bgu_raw = sb("bgu_raw", [P, NG * 2 * P])
        tile_hi = {n: sb(f"{n}_hi", [P, 256 if n == "a" else 512], F32R) for n in "pqbda"}
        tile_lo = {n: sb(f"{n}_lo", [P, 256 if n == "a" else 512], F32R) for n in "pqbda"}
        x_raw = sb("x_raw", [P, KT, TOK])
        x_hi = sb("x_hi", [P, KT, TOK], F32R)
        x_lo = sb("x_lo", [P, KT, TOK], F32R)
        x1_raw = sb("x1_raw", [P, KT, TOK])
        x1_parts = sb("x1_parts", [P, KT, 2, TOK], F32R)
        silu_sb = sb("silu_sb", [P, TOK])
        h_raw = sb("h_raw", [P, TOK])
        h_hi = [sb(f"h_hi{i}", [P, TOK], F32R) for i in range(2)]
        h_lo = [sb(f"h_lo{i}", [P, TOK], F32R) for i in range(2)]
        t_raw = sb("t_raw", [P, TOK])
        t_hi = sb("t_hi", [P, TOK], F32R)
        t_lo = sb("t_lo", [P, TOK], F32R)
        tgu_raw = [sb(f"tgu_raw{s}", [P, TOK]) for s in range(2)]
        tgu_hi = [sb(f"tgu_hi{s}", [P, TOK], F32R) for s in range(2)]
        tgu_lo = [sb(f"tgu_lo{s}", [P, TOK], F32R) for s in range(2)]
        ids_sb = sb("ids_sb", [1, 2 * NB * SPB], I32)
        group_sb = sb("group_sb", [P, 2, 2 * NB * NG], I32)
        seq_sb = sb("seq_sb", [P, 2, 2 * SPB], I32)
        row_b0 = sb("row_b0", [P, NG], I32)
        row_bd = sb("row_bd", [P, NG], I32)
        row_bgu = sb("row_bgu", [P, NG], I32)

        out_bank = [bank(f"out_bank{m}") for m in range(KT)]
        gate_bank = bank("gate_bank")
        up_bank = bank("up_bank")
        rank_bank = bank("rank_bank")
        rankgu_bank = bank("rankgu_bank")

        ids_in = sem("ids_in")
        seq_in = sem("seq_in")
        group_in = sem("group_in")
        const_in = sem("const_in")
        x_first_in = sem("x_first_in")
        x_in = sem("x_in")
        w0_first_in = sem("w0_first_in")
        w0_in = sem("w0_in")
        wgu_in = sem("wgu_in")
        wd_in = sem("wd_in")
        a0_pool_in = sem("a0_pool_in")
        a0_in = sem("a0_in")
        agu_pool_in = sem("agu_pool_in")
        agu_in = sem("agu_in")
        ad_pool_in = sem("ad_pool_in")
        ad_in = sem("ad_in")
        bwide_in = sem("bwide_in")
        bgu_in = sem("bgu_in")
        out_done = sem("out_done")
        hi_ready = {n: sem(f"{n}_hi_ready") for n in "pqbda"}
        lo_ready = {n: sem(f"{n}_lo_ready") for n in "pqbda"}
        tile_used = {n: sem(f"{n}_used") for n in "pqa"}
        x_hi_ready = sem("x_hi_ready")
        x_lo_ready = sem("x_lo_ready")
        l0_done = sem("l0_done")
        x1_raw_ready = sem("x1_raw_ready")
        x1_hi_ready = sem("x1_hi_ready")
        x1_lo_ready = sem("x1_lo_ready")
        rankgu_done = sem("rankgu_done")
        rank_lo_ready = sem("rank_lo_ready")
        ranksum_ready = sem("ranksum_ready")
        tgu_raw_ready = sem("tgu_raw_ready")
        tgu_hi_ready = sem("tgu_hi_ready")
        tgu_lo_ready = sem("tgu_lo_ready")
        rankd_done = sem("rankd_done")
        t_raw_ready = sem("t_raw_ready")
        t_hi_ready = sem("t_hi_ready")
        t_lo_ready = sem("t_lo_ready")
        gate_done = sem("gate_done")
        up_done = sem("up_done")
        silu_ready = sem("silu_ready")
        h_raw_ready = sem("h_raw_ready")
        h_hi_ready = sem("h_hi_ready")
        h_lo_ready = sem("h_lo_ready")
        hrow_hi_ready = sem("hrow_hi_ready")
        hrow_lo_ready = sem("hrow_lo_ready")
        down_done = sem("down_done")
        fin_done = sem("fin_done")
        bank_free = sem("bank_free")
        row_ready = sem("row_ready")
        zeroed = sem("zeroed")
        sp_passed = sem("sp_passed")
        pool_passed = sem("pool_passed")

        block = ctx.enter_context(nc.Block())

        @block.sync
        def _(sp):
            def gather(table, dst, arrived, first, n0=0, n1=SPB):
                width = table.shape[2]
                sp.sem_inc(sp_passed)
                with sp.Fori(n0 // 2, n1 // 2) as pair:
                    for i in range(2):
                        a = sp.value_load(ids_sb[0:1, ds(pair * 2 + (first + i), 1)], min_val=0,
                                          max_val=table.shape[0] - 1)
                        sp.dma_start(dst[:, ds(pair * (2 * width) + i * width, width)],
                                     table[ds(a, 1)].rearrange("a p c -> p (a c)")).then_inc(arrived, 16)

            l1 = NB * SPB
            a0_tab = a0.rearrange("(a p) c -> a p c", p=P)
            a0_flat = a0_raw[:].rearrange("p s k r -> p (s k r)")
            agu_flat = agu_raw[:].rearrange("p s g k r -> p (s g k r)")
            ad_flat = ad_raw[:].rearrange("p s j r -> p (s j r)")

            sp.dma_start(seq_sb[:], seq_rows).then_inc(seq_in, 16)
            sp.dma_start(ids_sb[:], ids).then_inc(ids_in, 16)
            sp.dma_start(group_sb[:], group_rows).then_inc(group_in, 16)
            sp.wait_ge(ids_in, 16)
            gather(a0_tab, a0_flat, a0_in, 0, POOL_A0)
            gather(agu, agu_flat, agu_in, l1, POOL_AGU + ACT_AGU)
            sp.dma_start(wgu_raw[:, 0:2, :], wgu[:, 0:2, :]).then_inc(wgu_in, 16)
            sp.dma_start(wd_raw[:, 0, :], wd[:, 0, :]).then_inc(wd_in, 16)
            for j in range(1, J):
                sp.wait_ge(wgu_in, 16 * j)
                sp.dma_start(wgu_raw[:, 2 * j:2 * j + 2, :], wgu[:, 2 * j:2 * j + 2, :]).then_inc(wgu_in, 16)
                if j == 1:
                    gather(ad, ad_flat, ad_in, l1, POOL_AD)
                sp.wait_ge(wd_in, 16 * j)
                sp.dma_start(wd_raw[:, j, :], wd[:, j, :]).then_inc(wd_in, 16)

            def store(b, m):
                sp.wait_ge(bank_free, KT + KT * b + m + 1)
                sp.sem_inc(sp_passed)
                sp.dma_start(outT[ds(b, 1), :, m].rearrange("b p t -> p (b t)"),
                             x1_raw[:, m, :]).then_inc(out_done, 16)

            def load_next(b):
                sp.wait_ge(x1_raw_ready, KT * (b + 1))
                sp.sem_inc(sp_passed)
                sp.dma_start(x_raw[:], xT[ds(b + 1, 1)].rearrange("b p k t -> p (b k) t")).then_inc(x_in, 16)
                sp.wait_ge(lo_ready["a"], NA * b + KT)
                gather(a0_tab, a0_flat, a0_in, (b + 1) * SPB)
                sp.wait_ge(hrow_lo_ready, 2 * (b + 1))
                sp.sem_inc(sp_passed)
                sp.wait_ge(lo_ready["p"], NP * b + 3)
                sp.wait_ge(lo_ready["q"], NQ * b + 3)
                gather(agu, agu_flat, agu_in, (b + 1) * SPB + l1)
                for m in range(KT):
                    store(b, m)
                sp.wait_ge(lo_ready["q"], NQ * (b + 1))
                gather(ad, ad_flat, ad_in, (b + 1) * SPB + l1)

            load_next(0)
            with sp.Fori(1, NB - 1) as b:
                load_next(b)
            for m in range(KT):
                store(NB - 1, m)
            sp.wait_ge(out_done, 16 * NB * KT)

        @block.gpsimd
        def _(pool):
            def gather(dst, arrived, table, rows):
                nc.gpsimd.indirect_dma_start(dst, None, table, bass.IndirectOffsetOnAxis(rows.bitcast(U32), 0)
                                             ).then_inc(arrived, 16)

            agu_rows = agu.rearrange("a p c -> (a p) c")
            ad_rows = ad.rearrange("a p c -> (a p) c")

            def gather_wide(table, rows):
                for g in range(NG):
                    gather(bwide_raw[:, g, :], bwide_in, table, rows[:, g:g + 1])

            def gather_gu():
                for g in range(NG):
                    gather(bgu_raw[:, g * 2 * P:(g + 1) * 2 * P], bgu_in, bgu, row_bgu[:, g:g + 1])

            steps = 3 + (J - 1)

            def body(b):
                wait_after(pool, bgu_in, 16 * NG * J * b)
                wait_after(pool, bwide_in, 32 * NG * b)
                pool.sem_inc(pool_passed)
                for rows, first in ((row_b0, 0), (row_bgu, NB * NG), (row_bd, NB * NG)):
                    nc.gpsimd.tensor_copy(rows[:], group_sb[:, 0, ds(b * NG + first, NG)]).then_inc(row_ready, 1)
                pool.wait_ge(row_ready, 2 + steps * b + 3)
                wait_after(pool, lo_ready["b"], NB_ * b)
                wait_after(pool, lo_ready["d"], ND * b)
                pool.sem_inc(pool_passed)
                gather_wide(b0, row_b0)
                if isinstance(b, int) and b == 0:
                    for i in range(POOL_AGU):
                        gather(agu_raw[:, i].rearrange("p g k r -> p (g k r)"), agu_pool_in, agu_rows,
                               seq_sb[:, 0, SPB + i:SPB + i + 1])
                gather_gu()
                pool.wait_ge(lo_ready["b"], NB_ * b + 1)
                pool.wait_ge(lo_ready["d"], ND * b + 1)
                pool.sem_inc(pool_passed)
                gather_wide(bd, row_bd)
                if isinstance(b, int) and b == 0:
                    for i in range(POOL_AD):
                        gather(ad_raw[:, i].rearrange("p j r -> p (j r)"), ad_pool_in, ad_rows,
                               seq_sb[:, 0, SPB + i:SPB + i + 1])
                with pool.Fori(1, J) as j:
                    pool.wait_ge(bgu_in, 16 * NG * J * b + 16 * NG * j)
                    pool.sem_inc(pool_passed)
                    nc.gpsimd.tensor_scalar(row_bgu[:], row_bgu[:], float(bd.shape[0]), None,
                                            ALU.add).then_inc(row_ready, 1)
                    pool.wait_ge(row_ready, 2 + steps * b + 3 + j)
                    pool.wait_ge(lo_ready["b"], NB_ * b + 1 + j)
                    pool.sem_inc(pool_passed)
                    gather_gu()

            pool.wait_ge(row_ready, 1)
            for i in range(POOL_A0):
                gather(a0_raw[:, i].rearrange("p k r -> p (k r)"), a0_pool_in, a0, seq_sb[:, 0, i:i + 1])
            pool.wait_ge(row_ready, 2)
            body(0)
            with pool.Fori(1, NB) as b:
                body(b)

        def a0_cols(k):
            return a0_raw[:, :, k, :]

        def rank_part(g, part):
            bank_g = (rankgu_bank, rank_bank)[g]
            return bank_g[:].rearrange("p (q part t) -> p q part t", q=2, part=2)[:, :, part, :]

        def group_cols(t, g):
            return t[:, g * GT:(g + 1) * GT].rearrange("p (q t) -> p q t", q=2)

        def a0_tile(b, k):
            if k == 0 or not (isinstance(b, int) and b == 0):
                return tile_hi["a"][:], tile_lo["a"][:]
            w = SPB * R
            n, c = divmod((k - 1) * w, 2 * w)
            return h_hi[n][:, c:c + w], h_lo[n][:, c:c + w]

        def ranks_of(t):
            return t.rearrange("p (s r) -> p s r", r=R)

        def agu_cols(k, s):
            return agu_raw[:, :, s, k, :].rearrange("p (q c) r -> p q c r", c=4)

        def agu_place(t, s):
            return t[:].rearrange("p (q g c r) -> p q g c r", q=4, g=2, r=R)[:, :, s]

        def small_place(t):
            return t[:, 0:SPB * R].rearrange("p (s r) -> p s r", r=R)

        def ad_cols(j):
            if isinstance(j, int):
                return ad_raw[:, :, j, :]
            return ad_raw[:, :, ds(j, 1), :].rearrange("p s j r -> p s (j r)")

        def wd_cols(j):
            return wd_raw[:, j, :] if isinstance(j, int) else wd_raw[:, ds(j, 1), :].rearrange("p j n -> p (j n)")

        def wgu_cols(j, s):
            if isinstance(j, int):
                return wgu_raw[:, 2 * j + s, :]
            return wgu_raw[:, ds(j * 2 + s, 1), :].rearrange("p j n -> p (j n)")

        @block.scalar
        def _(act):
            def split(n, src, place=None):
                dst = tile_hi[n][:] if place is None else place(tile_hi[n])
                return nc.scalar.copy(dst, src)

            def x_split(b, k):
                nc.scalar.copy(x_hi[:, k, :], x_raw[:, k, :]).then_inc(x_hi_ready, 1)

            def gu_rows(dst, k, ready):
                for s in range(2):
                    last_one = nc.scalar.copy(agu_place(dst, s), agu_cols(k, s))
                last_one.then_inc(ready, 1)

            def silu(b, j):
                n = J * b + j
                act.wait_ge(gate_done, n + 1)
                wait_after(act, h_raw_ready, n)
                nc.scalar.activation(silu_sb[:], gate_bank[:], ACT.Silu).then_inc(silu_ready, 1)

            def next_gate(b, j):
                act.wait_ge(wgu_in, 16 * (j + 1))
                act.wait_ge(tile_used["p"], UP_ * b + 3 + j)
                split("p", wgu_cols(j, 0)).then_inc(hi_ready["p"], 1)

            def next_up(b, j):
                if isinstance(j, int) and j == 0:
                    act.wait_ge(rankgu_done, b + 1)
                else:
                    act.wait_ge(tile_used["q"], UQ_ * b + 2 + j)
                split("q", wgu_cols(j, 1)).then_inc(hi_ready["q"], 1)

            def next_b_rows(b, j):
                act.wait_ge(bgu_in, 16 * NG * J * b + 16 * NG * (j + 1))
                split("b", bgu_raw[:]).then_inc(hi_ready["b"], 1)

            def h_split(b, j, last):
                act.wait_ge(h_raw_ready, J * b + j + 1)
                nc.scalar.copy(h_hi[last][:], h_raw[:]).then_inc(h_hi_ready, 1)

            def tile_step(b, j):
                if isinstance(j, int) and j == 0:
                    next_gate(b, 1)
                    silu(b, 0)
                else:
                    silu(b, j)
                    next_gate(b, j + 1)
                next_up(b, j + 1)
                act.wait_ge(up_done, J * b + j + 1)
                next_b_rows(b, j + 1)
                wait_after(act, down_done, J * b + j)
                act.wait_ge(l0_done, KT * (b + 1))
                act.wait_ge(rankgu_done, b + 1)
                h_split(b, j, 0)
                act.wait_ge(wd_in, 16 * (j + 1))
                split("d", wd_cols(j)).then_inc(hi_ready["d"], 1)
                if isinstance(b, int) and b == 0 and isinstance(j, int):
                    act.wait_ge(ad_pool_in, 16 * POOL_AD)
                act.wait_ge(ad_in, 16 * (SPB * (b + 1) - POOL_AD))
                act.wait_ge(tile_used["a"], UA_ * b + KT + j)
                split("a", ad_cols(j), small_place).then_inc(hi_ready["a"], 1)

            def body(b, last):
                first = isinstance(b, int) and b == 0

                def a0_rows(k):
                    if not first:
                        act.wait_ge(tile_used["a"], UA_ * b + k)
                    nc.scalar.copy(ranks_of(a0_tile(b, k)[0]), a0_cols(k)).then_inc(hi_ready["a"], 1)

                def b0_rows():
                    act.wait_ge(bwide_in, 32 * NG * b + 16 * NG)
                    split("b", bwide_raw[:, 0, :]).then_inc(hi_ready["b"], 1)
                    split("d", bwide_raw[:, 1, :]).then_inc(hi_ready["d"], 1)

                def w0_rows(n, k):
                    act.wait_ge(tile_used[n], (UP_ if n == "p" else UQ_) * b + 1)
                    split(n, w0_raw[:, k, :]).then_inc(hi_ready[n], 1)

                def ranks_split():
                    act.wait_ge(t_raw_ready, 2 * b + 1)
                    nc.scalar.copy(t_hi[:], t_raw[:]).then_inc(t_hi_ready, 1)

                if first:
                    for i in range(ACT_AGU):
                        s = POOL_AGU + i
                        a = act.value_load(ids_sb[0:1, NB * SPB + s:NB * SPB + s + 1], min_val=0,
                                           max_val=agu.shape[0] - 1)
                        act.dma_start(agu_raw[:, s].rearrange("p g k r -> p (g k r)"),
                                      agu[ds(a, 1)].rearrange("a p c -> p (a c)")).then_inc(agu_in, 16)
                        if i == 0:
                            w0_rows("p", 2)
                    w0_rows("q", 3)
                    act.wait_ge(a0_pool_in, 16 * POOL_A0)
                    act.wait_ge(a0_in, 16 * (SPB - POOL_A0))
                    for k in range(KT):
                        a0_rows(k)
                    b0_rows()
                    ranks_split()
                    act.wait_ge(agu_pool_in, 16 * POOL_AGU)
                else:
                    a0_rows(1)
                    w0_rows("p", 2)
                    a0_rows(2)
                    b0_rows()
                    a0_rows(3)
                    w0_rows("q", 3)
                    ranks_split()
                act.wait_ge(agu_in, 16 * (SPB * (b + 1) - POOL_AGU))
                wait_after(act, down_done, J * b)

                def x1_split(m):
                    act.wait_ge(x1_raw_ready, KT * b + m + 1)
                    nc.scalar.copy(x1_parts[:, m, 0, :], x1_raw[:, m, :]).then_inc(x1_hi_ready, 1)

                if first:
                    act.wait_ge(tile_used["a"], KT)
                    act.wait_ge(tile_used["p"], 2)
                    gu_rows(tile_hi["p"], 0, hi_ready["p"])
                    x1_split(0)
                    gu_rows(h_hi[0], 1, hrow_hi_ready)
                    x1_split(1)
                    gu_rows(h_hi[1], 2, hrow_hi_ready)
                    x1_split(2)
                    act.wait_ge(tile_used["q"], 2)
                    gu_rows(tile_hi["q"], 3, hi_ready["q"])
                    x1_split(3)
                else:
                    gu_rows(h_hi[0], 1, hrow_hi_ready)
                    gu_rows(h_hi[1], 2, hrow_hi_ready)
                    act.wait_ge(tile_used["p"], UP_ * b + 2)
                    gu_rows(tile_hi["p"], 0, hi_ready["p"])
                    for m in range(KT - 1):
                        x1_split(m)
                    act.wait_ge(tile_used["q"], UQ_ * b + 2)
                    gu_rows(tile_hi["q"], 3, hi_ready["q"])
                    x1_split(KT - 1)
                next_gate(b, 0)
                act.wait_ge(l0_done, KT * (b + 1))
                next_b_rows(b, 0)
                for g in range(NG):
                    act.wait_ge(rankgu_done, b + 1)
                    nc.scalar.copy(group_cols(silu_sb, g), rank_part(g, 1)).then_inc(rank_lo_ready, 1)
                next_up(b, 0)
                for s in range(2):
                    act.wait_ge(tgu_raw_ready, 2 * b + s + 1)
                    nc.scalar.copy(tgu_hi[s][:], tgu_raw[s][:]).then_inc(tgu_hi_ready, 1)
                tile_step(b, 0)
                with act.Fori(1, J - 1) as j:
                    tile_step(b, j)
                silu(b, J - 1)
                act.wait_ge(wd_in, 16 * J)
                act.wait_ge(tile_used["p"], UP_ * (b + 1))
                split("p", wd_cols(J - 1)).then_inc(hi_ready["p"], 1)
                if not last:
                    act.wait_ge(x_in, 16 * (b + 2))
                    act.wait_ge(l0_done, KT * (b + 1))
                    for k in range(KT):
                        x_split(b + 1, k)
                act.wait_ge(tile_used["q"], UQ_ * (b + 1))
                split("q", ad_cols(J - 1), small_place).then_inc(hi_ready["q"], 1)
                h_split(b, J - 1, 1)
                act.wait_ge(bwide_in, 32 * NG * (b + 1))
                act.wait_ge(up_done, J * (b + 1))
                split("b", bwide_raw[:, 0, :]).then_inc(hi_ready["b"], 1)
                act.wait_ge(down_done, J * b + J - 1)
                split("d", bwide_raw[:, 1, :]).then_inc(hi_ready["d"], 1)
                act.wait_ge(t_raw_ready, 2 * b + 2)
                act.wait_ge(l0_done, KT * (b + 1))
                nc.scalar.copy(t_hi[:], t_raw[:]).then_inc(t_hi_ready, 1)
                if not last:
                    act.wait_ge(down_done, J * (b + 1))
                    split("p", w0_raw[:, 0, :]).then_inc(hi_ready["p"], 1)
                    act.wait_ge(a0_in, 16 * (SPB * (b + 2) - POOL_A0))
                    act.wait_ge(tile_used["a"], UA_ * (b + 1))
                    split("a", a0_cols(0), small_place).then_inc(hi_ready["a"], 1)
                    split("q", w0_raw[:, 1, :]).then_inc(hi_ready["q"], 1)

            act.wait_ge(zeroed, 1)
            nc.scalar.activation(silu_sb[:, 0:1], tgu_raw[0][:, 0:1], ACT.Silu)
            head = 1
            act.dma_start(x_raw[:, 0:head, :], xT[0, :, 0:head]).then_inc(x_first_in, 16)
            act.dma_start(w0_raw[:, 0:head, :], w0[:, 0:head]).then_inc(w0_first_in, 16)
            act.dma_start(x_raw[:, head:, :], xT[0, :, head:]).then_inc(x_in, 16)
            act.dma_start(w0_raw[:, head:, :], w0[:, head:]).then_inc(w0_in, 16)
            act.wait_ge(x_first_in, 16)
            x_split(0, 0)
            act.wait_ge(w0_first_in, 16)
            split("p", w0_raw[:, 0, :]).then_inc(hi_ready["p"], 1)
            act.dma_start(mask_sb[:], mask).then_inc(const_in, 16)
            act.dma_start(bias_sb[:], bias).then_inc(const_in, 16)
            act.wait_ge(x_in, 16)
            x_split(0, 1)
            x_split(0, 2)
            act.wait_ge(w0_in, 16)
            split("q", w0_raw[:, 1, :]).then_inc(hi_ready["q"], 1)
            x_split(0, 3)
            act.wait_ge(ids_in, 16)
            body(0, False)
            with act.Fori(1, NB - 1) as b:
                body(b, False)
            body(NB - 1, True)

        @block.vector
        def _(dve):
            def rest(n, src, place=None, count=None):
                dst, hi = (tile_lo[n][:], f32(tile_hi[n][:])) if place is None else \
                    (place(tile_lo[n]), f32(place(tile_hi[n])))
                dve.wait_ge(hi_ready[n], count)
                return nc.vector.tensor_tensor(dst, src, hi, ALU.subtract)

            def x_rest(b, k):
                dve.wait_ge(x_hi_ready, KT * b + k + 1)
                nc.vector.tensor_tensor(x_lo[:, k, :], x_raw[:, k, :], f32(x_hi[:, k, :]),
                                        ALU.subtract).then_inc(x_lo_ready, 1)

            def gu_rows(lo, hi, k, made, count, ready):
                dve.wait_ge(made, count)
                for s in range(2):
                    last_one = nc.vector.tensor_tensor(agu_place(lo, s), agu_cols(k, s), f32(agu_place(hi, s)),
                                                       ALU.subtract)
                last_one.then_inc(ready, 1)

            def h_product(b, j):
                n = J * b + j
                dve.wait_ge(silu_ready, n + 1)
                dve.wait_ge(up_done, n + 1)
                wait_after(dve, h_lo_ready, n)
                nc.vector.tensor_tensor(h_raw[:], up_bank[:], silu_sb[:], ALU.mult).then_inc(h_raw_ready, 1)

            def h_rest(b, j, last):
                dve.wait_ge(h_hi_ready, J * b + j + 1)
                nc.vector.tensor_tensor(h_lo[last][:], h_raw[:], f32(h_hi[last][:]),
                                        ALU.subtract).then_inc(h_lo_ready, 1)

            def t_rest(n):
                dve.wait_ge(t_hi_ready, n)
                nc.vector.tensor_tensor(t_lo[:], t_raw[:], f32(t_hi[:]), ALU.subtract).then_inc(t_lo_ready, 1)

            def x1_sum(b, m):
                dve.wait_ge(l0_done, KT * b + m + 1)
                nc.vector.scalar_tensor_tensor(x1_raw[:, m, :], out_bank[m][:], bias_sb[:, m:m + 1],
                                               x_raw[:, m, :], ALU.add, ALU.add).then_inc(x1_raw_ready, 1)

            def x1_rest(b, m):
                dve.wait_ge(x1_hi_ready, KT * b + m + 1)
                nc.vector.tensor_tensor(x1_parts[:, m, 1, :], x1_raw[:, m, :], f32(x1_parts[:, m, 0, :]),
                                        ALU.subtract).then_inc(x1_lo_ready, 1)

            def final_sum(b, m):
                dve.wait_ge(fin_done, KT * b + m + 1)
                nc.vector.tensor_tensor(x1_raw[:, m, :], out_bank[m][:], x1_raw[:, m, :],
                                        ALU.add).then_inc(bank_free, 1)

            def tile_step(b, j):
                rest("p", wgu_cols(j + 1, 0), count=NP * b + 5 + j).then_inc(lo_ready["p"], 1)
                h_product(b, j)
                rest("q", wgu_cols(j + 1, 1), count=NQ * b + 5 + j).then_inc(lo_ready["q"], 1)
                rest("b", bgu_raw[:], count=NB_ * b + 3 + j).then_inc(lo_ready["b"], 1)
                h_rest(b, j, 0)
                rest("d", wd_cols(j), count=ND * b + 2 + j).then_inc(lo_ready["d"], 1)
                rest("a", ad_cols(j), small_place, NA * b + KT + 1 + j).then_inc(lo_ready["a"], 1)

            def body(b, last):
                def a0_rows(k):
                    hi, lo = a0_tile(b, k)
                    dve.wait_ge(hi_ready["a"], NA * b + k + 1)
                    nc.vector.tensor_tensor(ranks_of(lo), a0_cols(k), ranks_of(f32(hi)),
                                            ALU.subtract).then_inc(lo_ready["a"], 1)

                def b0_rows():
                    rest("b", bwide_raw[:, 0, :], count=NB_ * b + 1).then_inc(lo_ready["b"], 1)
                    rest("d", bwide_raw[:, 1, :], count=ND * b + 1).then_inc(lo_ready["d"], 1)

                def ranks():
                    dve.wait_ge(tile_used["a"], UA_ * b + KT)
                    wait_after(dve, t_lo_ready, 2 * b)
                    nc.vector.tensor_tensor(t_raw[:], rank_bank[:], mask_sb[:], ALU.mult).then_inc(t_raw_ready, 1)
                    t_rest(2 * b + 1)

                first = isinstance(b, int) and b == 0
                def w0_rest(n, k):
                    rest(n, w0_raw[:, k, :], count=(NP if n == "p" else NQ) * b + 2).then_inc(lo_ready[n], 1)

                if first:
                    w0_rest("p", 2)
                    w0_rest("q", 3)
                    for k in range(KT):
                        a0_rows(k)
                    b0_rows()
                    dve.wait_ge(const_in, 32)
                else:
                    a0_rows(1)
                    w0_rest("p", 2)
                    a0_rows(2)
                    b0_rows()
                    a0_rows(3)
                    w0_rest("q", 3)
                ranks()

                def gu_row(k):
                    if k in (0, 3):
                        n, count = ("p", NP * b + 3) if k == 0 else ("q", NQ * b + 3)
                        gu_rows(tile_lo[n], tile_hi[n], k, hi_ready[n], count, lo_ready[n])
                    else:
                        gu_rows(h_lo[k - 1], h_hi[k - 1], k, hrow_hi_ready, 2 * b + k, hrow_lo_ready)

                if first:
                    x1_sum(b, 0)
                    x1_sum(b, 1)
                    gu_row(0)
                    x1_rest(b, 0)
                    gu_row(1)
                    x1_sum(b, 2)
                    x1_rest(b, 1)
                    gu_row(2)
                    x1_sum(b, 3)
                else:
                    gu_row(1)
                    gu_row(2)
                    wait_after(dve, out_done, 16 * KT * b)
                    x1_sum(b, 0)
                    gu_row(0)
                    x1_sum(b, 1)
                    x1_rest(b, 0)
                    x1_sum(b, 2)
                    x1_rest(b, 1)
                    x1_sum(b, 3)
                x1_rest(b, 2)
                x1_rest(b, 3)
                gu_row(3)
                rest("p", wgu_cols(0, 0), count=NP * b + 4).then_inc(lo_ready["p"], 1)
                rest("b", bgu_raw[:], count=NB_ * b + 2).then_inc(lo_ready["b"], 1)
                dve.wait_ge(rankgu_done, b + 1)
                wait_after(dve, tgu_lo_ready, 2 * b)
                for g in range(NG):
                    dve.wait_ge(rank_lo_ready, NG * b + g + 1)
                    nc.vector.tensor_tensor(group_cols(h_raw, g), rank_part(g, 0), group_cols(silu_sb, g),
                                            ALU.add).then_inc(ranksum_ready, 1)
                rest("q", wgu_cols(0, 1), count=NQ * b + 4).then_inc(lo_ready["q"], 1)
                dve.wait_ge(ranksum_ready, 2 * b + 2)
                for s in range(2):
                    for odd in range(2):
                        rows, own = slice(64 * s, 64 * s + 64), slice(64 * odd, 64 * odd + 64)
                        cols = lambda t, h: t.rearrange("p (g h t) -> p g h t", h=2, t=P)[:, :, h, :]
                        last_one = nc.vector.scalar_tensor_tensor(
                            cols(tgu_raw[s][own, :], odd), cols(h_raw[rows, :], odd), SCALE,
                            cols(mask_sb[rows, :], s), ALU.mult, ALU.mult)
                    last_one.then_inc(tgu_raw_ready, 1)
                for s in range(2):
                    dve.wait_ge(tgu_hi_ready, 2 * b + s + 1)
                    nc.vector.tensor_tensor(tgu_lo[s][:], tgu_raw[s][:], f32(tgu_hi[s][:]),
                                            ALU.subtract).then_inc(tgu_lo_ready, 1)
                tile_step(b, 0)
                with dve.Fori(1, J - 1) as j:
                    tile_step(b, j)

                rest("p", wd_cols(J - 1), count=NP * (b + 1)).then_inc(lo_ready["p"], 1)
                if not last:
                    for k in range(KT):
                        x_rest(b + 1, k)
                h_product(b, J - 1)
                rest("q", ad_cols(J - 1), small_place, NQ * (b + 1)).then_inc(lo_ready["q"], 1)
                h_rest(b, J - 1, 1)
                rest("b", bwide_raw[:, 0, :], count=NB_ * (b + 1)).then_inc(lo_ready["b"], 1)
                dve.wait_ge(rankd_done, b + 1)
                dve.wait_ge(t_lo_ready, 2 * b + 1)
                nc.vector.scalar_tensor_tensor(t_raw[:], rank_bank[:], SCALE, mask_sb[:],
                                               ALU.mult, ALU.mult).then_inc(t_raw_ready, 1)
                rest("d", bwide_raw[:, 1, :], count=ND * (b + 1)).then_inc(lo_ready["d"], 1)
                t_rest(2 * b + 2)
                if not last:
                    rest("p", w0_raw[:, 0, :], count=NP * (b + 1) + 1).then_inc(lo_ready["p"], 1)
                final_sum(b, 0)
                final_sum(b, 1)
                if not last:
                    rest("a", a0_cols(0), small_place, NA * (b + 1) + 1).then_inc(lo_ready["a"], 1)
                final_sum(b, 2)
                final_sum(b, 3)
                if not last:
                    rest("q", w0_raw[:, 1, :], count=NQ * (b + 1) + 1).then_inc(lo_ready["q"], 1)

            for s in range(2):
                nc.vector.memset(tgu_raw[s][:], 0.0).then_inc(zeroed, 1)
            nc.vector.memset(t_raw[:, 0:1], 0.0).then_inc(bank_free, KT)
            for t, rows, arrived in ((seq_sb, P, seq_in), (group_sb, R, group_in)):
                dve.wait_ge(arrived, 16)
                nc.vector.scalar_tensor_tensor(t[:, 0], t[:, 0], float(rows), t[:, 1],
                                               ALU.mult, ALU.add).then_inc(row_ready, 1)
            dve.wait_ge(zeroed, 2)
            x_rest(0, 0)
            rest("p", w0_raw[:, 0, :], count=1).then_inc(lo_ready["p"], 1)
            x_rest(0, 1)
            x_rest(0, 2)
            rest("q", w0_raw[:, 1, :], count=1).then_inc(lo_ready["q"], 1)
            x_rest(0, 3)
            body(0, False)
            with dve.Fori(1, NB - 1) as b:
                body(b, False)
            body(NB - 1, True)

        @block.tensor
        def _(pe):
            def mm3(out, w_hi, w_lo, v_hi, v_lo, start=False, stop=False):
                nc.tensor.matmul(out, w_lo, v_hi, start=start, stop=False, skip_group_check=True)
                nc.tensor.matmul(out, w_hi, v_lo, start=False, stop=False, skip_group_check=True)
                return nc.tensor.matmul(out, w_hi, v_hi, start=False, stop=stop, skip_group_check=True)

            def group(g):
                return slice(g * GT, (g + 1) * GT)

            def col(n, c, w=P):
                return tile_hi[n][:, c:c + w], tile_lo[n][:, c:c + w]

            def gate_up(b, j):
                banks = (gate_bank, up_bank)

                def weights(s):
                    n = "pq"[s]
                    pe.wait_ge(lo_ready[n], (NP, NQ)[s] * b + 4 + j)
                    wait_after(pe, (silu_ready, h_raw_ready)[s], J * b + j)
                    for k in range(KT):
                        last_one = mm3(banks[s][:], *col(n, k * P), x1_parts[:, k, 0, :], x1_parts[:, k, 1, :],
                                       start=(k == 0))
                    last_one.then_inc(tile_used[n], 1)

                def ranks(s):
                    pe.wait_ge(lo_ready["b"], NB_ * b + 2 + j)
                    pe.wait_ge(tgu_lo_ready, 2 * b + s + 1)
                    for g in range(NG):
                        last_one = mm3(banks[s][:, group(g)], *col("b", (2 * g + s) * P),
                                       tgu_hi[s][:, group(g)], tgu_lo[s][:, group(g)], stop=(g == NG - 1))
                    last_one.then_inc((gate_done, up_done)[s], 1)

                for step, s in ((weights, 0), (weights, 1), (ranks, 0), (ranks, 1)) if isinstance(j, int) and j == 0 \
                        else ((weights, 0), (ranks, 0), (weights, 1), (ranks, 1)):
                    step(s)

            def down(b, j, first, last):
                a, w = ("q", "p") if last else ("a", "d")
                pe.wait_ge(h_lo_ready, J * b + j + 1)
                if last:
                    pe.wait_ge(lo_ready["q"], NQ * (b + 1))
                else:
                    pe.wait_ge(lo_ready["a"], NA * b + KT + 1 + j)
                for g in range(NG):
                    last_one = mm3(rank_bank[:, group(g)], *col(a, g * P), h_hi[last][:, group(g)],
                                   h_lo[last][:, group(g)], start=(first and g == 0), stop=bool(last and g == NG - 1))
                last_one.then_inc(rankd_done if last else tile_used["a"], 1)
                if last:
                    pe.wait_ge(lo_ready["p"], NP * (b + 1))
                else:
                    pe.wait_ge(lo_ready["d"], ND * b + 2 + j)
                for m in range(KT):
                    last_one = mm3(out_bank[m][:], *col(w, m * P), h_hi[last][:], h_lo[last][:], start=first)
                last_one.then_inc(down_done, 1)

            def b_rows(m, done):
                for g, n in enumerate("bd"):
                    last_one = mm3(out_bank[m][:, group(g)], *col(n, m * P), t_hi[:, group(g)],
                                   t_lo[:, group(g)], stop=(g == NG - 1))
                last_one.then_inc(done, 1)

            def w0_rows(b, k, tiles):
                n = "pq"[k % 2]
                pe.wait_ge(x_lo_ready, KT * b + k + 1)
                pe.wait_ge(lo_ready[n], (NP if n == "p" else NQ) * b + k // 2 + 1)
                for m in tiles:
                    if k == 0:
                        pe.wait_ge(bank_free, KT * b + m + 1)
                    last_one = mm3(out_bank[m][:], *col(n, m * P), x_hi[:, k, :], x_lo[:, k, :], start=(k == 0))
                if tiles[-1] == KT - 1:
                    last_one.then_inc(tile_used[n], 1)

            def ranks0(b, k):
                pe.wait_ge(lo_ready["a"], NA * b + k + 1)
                hi, lo = a0_tile(b, k)
                for g in range(NG):
                    rows = slice(g * P, (g + 1) * P)
                    last_one = mm3(rank_bank[:, group(g)], hi[:, rows], lo[:, rows], x_hi[:, k, group(g)],
                                   x_lo[:, k, group(g)], start=(k == 0 and g == 0),
                                   stop=(k == KT - 1 and g == NG - 1))
                last_one.then_inc(tile_used["a"], 1)

            def body(b):
                def b_rows_here():
                    pe.wait_ge(lo_ready["b"], NB_ * b + 1)
                    pe.wait_ge(lo_ready["d"], ND * b + 1)
                    pe.wait_ge(t_lo_ready, 2 * b + 1)

                if isinstance(b, int) and b == 0:
                    w0_rows(b, 0, range(KT))
                    w0_rows(b, 1, range(KT))
                    w0_rows(b, 2, range(KT))
                    for k in range(KT):
                        ranks0(b, k)
                    w0_rows(b, 3, [0, 1, 2])
                    b_rows_here()
                    b_rows(0, l0_done)
                    w0_rows(b, 3, [3])
                    for m in range(1, KT):
                        b_rows(m, l0_done)
                else:
                    w0_rows(b, 0, [0, 1])
                    ranks0(b, 0)
                    w0_rows(b, 0, [2, 3])
                    ranks0(b, 1)
                    w0_rows(b, 1, [0, 1])
                    ranks0(b, 2)
                    w0_rows(b, 1, [2, 3])
                    ranks0(b, 3)
                    w0_rows(b, 2, range(KT))
                    for m in range(KT):
                        w0_rows(b, 3, [m])
                        if m == 0:
                            b_rows_here()
                        b_rows(m, l0_done)
                rows = [(tile_hi["p"], tile_lo["p"], lo_ready["p"], NP * b + 3),
                        (h_hi[0], h_lo[0], hrow_lo_ready, 2 * b + 1),
                        (h_hi[1], h_lo[1], hrow_lo_ready, 2 * b + 2),
                        (tile_hi["q"], tile_lo["q"], lo_ready["q"], NQ * b + 3)]
                for k, (hi, lo, made, count) in enumerate(rows):
                    pe.wait_ge(x1_lo_ready, KT * b + k + 1)
                    pe.wait_ge(made, count)
                    for q in range(TOK // P):
                        cols, place = slice(q * P, (q + 1) * P), (q % 2) * 2 * P
                        bank_q = (rankgu_bank, rank_bank)[q // 2]
                        nc.tensor.matmul(bank_q[:, place:place + 2 * P], hi[:, cols], x1_parts[:, k, :, cols],
                                         start=(k == 0 and q % 2 == 0), stop=False, skip_group_check=True)
                        last_one = nc.tensor.matmul(bank_q[:, place:place + P], lo[:, cols], x1_parts[:, k, 0, cols],
                                                    start=False, stop=(k == KT - 1 and q % 2 == 1),
                                                    skip_group_check=True)
                    if k == 0:
                        last_one.then_inc(tile_used["p"], 1)
                last_one.then_inc(rankgu_done, 1)
                gate_up(b, 0)
                gate_up(b, 1)
                down(b, 0, True, 0)
                with pe.Fori(2, J) as j:
                    gate_up(b, j)
                    down(b, j - 1, False, 0)
                down(b, J - 1, False, 1)
                pe.wait_ge(lo_ready["b"], NB_ * (b + 1))
                pe.wait_ge(lo_ready["d"], ND * (b + 1))
                pe.wait_ge(t_lo_ready, 2 * b + 2)
                for m in range(KT):
                    b_rows(m, fin_done)

            body(0)
            with pe.Fori(1, NB) as b:
                body(b)


def kernel(**inputs):
    import numpy as np
    import concourse.bacc as bacc
    from concourse.bass_utils import run_bass_kernel_spmd

    def tiles(w):
        return w.reshape(w.shape[0], -1, P).transpose(2, 1, 0)

    def pad(w, axis):
        widths = [(0, 0)] * w.ndim
        widths[axis] = (0, J * P - w.shape[axis])
        return np.pad(w, widths)

    v = {k: np.asarray(a) for k, a in inputs.items()}
    x = v["x"]
    nseq = x.shape[0]
    c = {n[len("L1_cond_"):]: a for n, a in v.items() if n.startswith("L1_cond_")}
    gate, up = (pad(c[n], 0).reshape(J, P, KT, P) for n in ("W_gate", "W_up"))
    a_gate, a_up = (c[n][0].reshape(-1, R, KT, P) for n in ("A_gate", "A_up"))
    b_gate, b_up = (pad(c[n][0], 1).reshape(-1, J, P, R) for n in ("B_gate", "B_up"))
    ids0, ids1 = v["itok_B_6_15"], v["itok_B_2_6"]
    place = np.arange(P, dtype=np.int32)[:, None]
    per_group = P // R
    own = np.arange(P)[:, None] // R == (np.arange(TOK)[None, :] // SEQ) % per_group
    arrays = {
        "xT": x.reshape(NB, TOK, KT, P).transpose(0, 3, 2, 1),
        "w0": tiles(v["L0_cond_base_weight"]),
        "bias": v["L0_cond_base_bias"].reshape(KT, P).T,
        "a0": v["L0_cond_lora_A_w"].reshape(-1, R, KT, P).transpose(0, 3, 2, 1).reshape(-1, KT * R),
        "b0": v["L0_cond_lora_B_w"].transpose(0, 2, 1).reshape(-1, H),
        "wgu": np.stack([gate, up]).transpose(4, 1, 0, 3, 2).reshape(P, J * 2, KT * P),
        "wd": tiles(pad(c["W_down"], 1)),
        "agu": np.stack([a_gate, a_up]).transpose(1, 4, 0, 3, 2).reshape(-1, P, 2 * KT * R),
        "bgu": np.stack([b_gate, b_up]).transpose(2, 1, 4, 0, 3).reshape(-1, 2 * P),
        "ad": pad(c["A_down"][0], 2).reshape(-1, R, J, P).transpose(0, 3, 2, 1).reshape(-1, P, J * R),
        "bd": c["B_down"][0].transpose(0, 2, 1).reshape(-1, H),
        "ids": np.concatenate([ids0, ids1]).reshape(1, -1),
        "seq_rows": np.stack([np.tile(np.concatenate([ids0[:SPB], ids1[:SPB]]), (P, 1)),
                              np.tile(place, (1, 2 * SPB))], axis=1),
        "group_rows": np.stack([np.repeat(np.concatenate([ids0, ids1]).reshape(-1, per_group), R, axis=1).T,
                                np.tile(place % R, (1, 2 * nseq // per_group))], axis=1),
        "mask": own.astype(np.float32),
    }
    nc = bacc.Bacc("TRN2", target_bir_lowering=False, num_devices=1)
    arrays = {f"{n}_dram": np.ascontiguousarray(a) for n, a in arrays.items()}
    aps = [nc.dram_tensor(n, a.shape, mybir.dt.from_np(a.dtype), kind="ExternalInput").ap() for n, a in arrays.items()]
    out = nc.dram_tensor("out_dram", (NB, P, KT, TOK), F32, kind="ExternalOutput").ap()
    lora_ffn_program(nc, *aps, out)
    r = run_bass_kernel_spmd(nc, [arrays], core_ids=[0])
    got = r.results[0]["out_dram"]
    return got.transpose(0, 3, 2, 1).reshape(x.shape)
```
